# Optimizing a Trainium2 kernel written in Bass

```python
import numpy as np
import jax
import jax.numpy as jnp

def _softmax(x, axis=-1):
    return jax.nn.softmax(x, axis=axis)

def _gelu(x):
    return jax.nn.gelu(x, approximate=True)

def _silu(x):
    return jax.nn.silu(x)

def _sigmoid(x):
    return jax.nn.sigmoid(x)

def _layernorm(x, axis=-1, eps=1e-05):
    m = jnp.mean(x, axis=axis, keepdims=True)
    v = jnp.var(x, axis=axis, keepdims=True)
    return (x - m) / jnp.sqrt(v + eps)

def _scatter_add(tgt, idx, src, axis=0):
    return tgt.at[idx].add(src)

def _segment_sum(src, seg, n):
    return jax.ops.segment_sum(src, seg, n)
kernel_name = 'mk_macaron_d1_jaxref_r8_f4b648'

def setup_inputs(seed: int=0):
    np.random.seed(seed)
    _w = jnp.asarray

    def _L0_attn_setup():
        import jax, jax.numpy as jnp
        import numpy as np
        EMBED_DIM = 128
        VALUE_DIM = 256
        NUM_HEADS = 8
        KEY_DIM = EMBED_DIM // NUM_HEADS
        HEAD_DIM = VALUE_DIM // NUM_HEADS
        EPS = 1e-05
        B, S = (2, 256)

        def _xavier(k, shape, gain):
            a = gain * np.sqrt(6.0 / (shape[0] + shape[1]))
            return jax.random.uniform(k, shape, jnp.float32, -a, a)

        def _rel_pos(slen):
            lin = jnp.linspace(0.0, 1.0, KEY_DIM // 2)
            angle = jnp.repeat(1.0 / 10000.0 ** lin, 2)
            decay = jnp.log1p(-2.0 ** (-5.0 - jnp.arange(NUM_HEADS, dtype=jnp.float32)))
            idx = jnp.arange(slen, dtype=jnp.float32)
            sin = jnp.sin(idx[:, None] * angle[None, :])
            cos = jnp.cos(idx[:, None] * angle[None, :])
            diff = idx[:, None] - idx[None, :]
            m = jnp.where(diff[None] >= 0, jnp.exp(diff[None] * decay[:, None, None]), 0.0)
            m = m / jnp.sqrt(m.sum(-1, keepdims=True))
            return (sin, cos, m)

        def _rotate_every_two(x):
            x1 = x[..., ::2]
            x2 = x[..., 1::2]
            return jnp.stack((-x2, x1), axis=-1).reshape(x.shape)
        key = jax.random.key(seed)
        ks = jax.random.split(key, 6)
        g = 2.0 ** (-2.5)
        return {'x': jax.random.normal(ks[0], (B, S, EMBED_DIM), jnp.float32), 'wq': _xavier(ks[1], (EMBED_DIM, EMBED_DIM), g), 'wk': _xavier(ks[2], (EMBED_DIM, EMBED_DIM), g), 'wv': _xavier(ks[3], (EMBED_DIM, VALUE_DIM), g), 'wg': _xavier(ks[4], (EMBED_DIM, VALUE_DIM), g), 'wo': _xavier(ks[5], (VALUE_DIM, EMBED_DIM), 1.0)}
    _L0_attn_in = _L0_attn_setup()

    def _L0_ffn_setup():
        import jax, jax.numpy as jnp
        import numpy as np
        B, N, D = (4, 256, 128)
        SPARSITY = 0.01
        key = jax.random.key(seed)
        k1, k2, k3 = jax.random.split(key, 3)
        x = jax.random.normal(k1, (B, N, D), dtype=jnp.float32)
        spatial = jax.random.normal(k2, (D, D), dtype=jnp.float32) * 0.02
        freq = jnp.fft.fft(spatial, axis=-1)
        k = int(D * SPARSITY)
        mag = jnp.abs(freq)
        kth = jax.lax.top_k(mag, k)[0][:, -1:]
        w_sparse = jnp.where(mag >= kth, freq, 0.0 + 0j)
        bias = jax.random.normal(k3, (D,), dtype=jnp.float32) * 0.01
        return {'x': x, 'w_freq_real': jnp.real(w_sparse).astype(jnp.float32), 'w_freq_imag': jnp.imag(w_sparse).astype(jnp.float32), 'bias': bias}
    _L0_ffn_in = _L0_ffn_setup()
    _d = {'L0_attn_x': _L0_attn_in['x'], 'L0_attn_wq': _L0_attn_in['wq'], 'L0_attn_wk': _L0_attn_in['wk'], 'L0_attn_wv': _L0_attn_in['wv'], 'L0_attn_wg': _L0_attn_in['wg'], 'L0_attn_wo': _L0_attn_in['wo'], 'L0_ffn_w_freq_real': _L0_ffn_in['w_freq_real'], 'L0_ffn_w_freq_imag': _L0_ffn_in['w_freq_imag'], 'L0_ffn_bias': _L0_ffn_in['bias']}
    _x0 = _d['L0_attn_x']
    _d['L0_attn_x'] = jax.random.normal(jax.random.fold_in(jax.random.key(seed), 1), (4, 1024, 128), dtype=_x0.dtype)
    del _x0
    return _d

def reference(L0_attn_x, L0_attn_wq, L0_attn_wk, L0_attn_wv, L0_attn_wg, L0_attn_wo, L0_ffn_w_freq_real, L0_ffn_w_freq_imag, L0_ffn_bias):

    def _L0_attn_ref(x, wq, wk, wv, wg, wo):
        import jax, jax.numpy as jnp
        import numpy as np
        EMBED_DIM = 128
        VALUE_DIM = 256
        NUM_HEADS = 8
        KEY_DIM = EMBED_DIM // NUM_HEADS
        HEAD_DIM = VALUE_DIM // NUM_HEADS
        EPS = 1e-05
        B, S = (2, 256)

        def _xavier(k, shape, gain):
            a = gain * np.sqrt(6.0 / (shape[0] + shape[1]))
            return jax.random.uniform(k, shape, jnp.float32, -a, a)

        def _rel_pos(slen):
            lin = jnp.linspace(0.0, 1.0, KEY_DIM // 2)
            angle = jnp.repeat(1.0 / 10000.0 ** lin, 2)
            decay = jnp.log1p(-2.0 ** (-5.0 - jnp.arange(NUM_HEADS, dtype=jnp.float32)))
            idx = jnp.arange(slen, dtype=jnp.float32)
            sin = jnp.sin(idx[:, None] * angle[None, :])
            cos = jnp.cos(idx[:, None] * angle[None, :])
            diff = idx[:, None] - idx[None, :]
            m = jnp.where(diff[None] >= 0, jnp.exp(diff[None] * decay[:, None, None]), 0.0)
            m = m / jnp.sqrt(m.sum(-1, keepdims=True))
            return (sin, cos, m)

        def _rotate_every_two(x):
            x1 = x[..., ::2]
            x2 = x[..., 1::2]
            return jnp.stack((-x2, x1), axis=-1).reshape(x.shape)
        b, s, _ = x.shape
        sin, cos, mask = _rel_pos(s)
        q = x @ wq
        k = x @ wk * KEY_DIM ** (-0.5)
        v = x @ wv
        g = x @ wg
        q = q.reshape(b, s, NUM_HEADS, KEY_DIM).transpose(0, 2, 1, 3)
        k = k.reshape(b, s, NUM_HEADS, KEY_DIM).transpose(0, 2, 1, 3)
        qr = q * cos + _rotate_every_two(q) * sin
        kr = k * cos + _rotate_every_two(k) * sin
        vr = v.reshape(b, s, NUM_HEADS, HEAD_DIM).transpose(0, 2, 1, 3)
        qk = jnp.einsum('bhik,bhjk->bhij', qr, kr) * mask[None]
        denom = jnp.clip(jnp.abs(jax.lax.stop_gradient(qk).sum(-1, keepdims=True)), 1.0, None)
        qk = qk / denom
        out = jnp.einsum('bhij,bhjd->bihd', qk, vr)
        out = out * jax.lax.rsqrt(jnp.mean(out * out, axis=-1, keepdims=True) + EPS)
        out = out.reshape(b, s, VALUE_DIM)
        out = jax.nn.silu(g) * out
        return out @ wo

    def _L0_ffn_ref(x, w_freq_real, w_freq_imag, bias):
        import jax, jax.numpy as jnp
        import numpy as np
        B, N, D = (4, 256, 128)
        SPARSITY = 0.01
        w = jax.lax.complex(w_freq_real, w_freq_imag)
        x_freq = jnp.fft.fft(x, axis=-1)
        y_freq = jnp.einsum('bnd,do->bno', x_freq, w)
        y = jnp.real(jnp.fft.ifft(y_freq, axis=-1))
        return y + bias
    x = L0_attn_x
    x = x + 0.5 * _L0_ffn_ref(_layernorm(x, axis=-1), L0_ffn_w_freq_real, L0_ffn_w_freq_imag, L0_ffn_bias)
    x = x + _L0_attn_ref(_layernorm(x, axis=-1), L0_attn_wq, L0_attn_wk, L0_attn_wv, L0_attn_wg, L0_attn_wo)
    x = x + 0.5 * _L0_ffn_ref(_layernorm(x, axis=-1), L0_ffn_w_freq_real, L0_ffn_w_freq_imag, L0_ffn_bias)
    return x

_drawn_inputs = setup_inputs


def setup_inputs(seed=0):
    import zlib

    import numpy as np

    out = dict(_drawn_inputs(seed))
    spreads = {}
    factors = {'L0_ffn_bias': 6.174}
    for name, (base, spread) in spreads.items():
        noise = np.random.default_rng([zlib.crc32(name.encode()), seed]).standard_normal(out[name].shape)
        drawn = base * np.exp(spread * noise) if base else spread * noise
        out[name] = jnp.asarray(drawn.astype(out[name].dtype))
    for name, factor in factors.items():
        out[name] = (out[name] * factor).astype(out[name].dtype)
    return out
```

```python
import numpy as np
import concourse.bass as bass
from concourse import mybir
from contextlib import ExitStack

BATCHES, SEQ, D = 4, 1024, 128
HEADS, KEY, VAL = 8, 16, 32
PAIRS = HEADS // 2
CHUNK = 128
CHUNKS = SEQ // CHUNK
TILES = BATCHES * CHUNKS
QK = 2 * HEADS * KEY
VW = HEADS * VAL
VA = VAL + 1
LN_EPS = 1e-5
RMS_EPS = 1e-5
STEP = BATCHES
DEPTH = 3

COS_M, SIN_M, NEG_SIN_M, CENTRE, IDENT, CAUSAL, BLOCK, PARITY = (
    slice(0, 128), slice(128, 256), slice(256, 384), slice(384, 512), slice(512, 640),
    slice(640, 768), slice(768, 768 + HEADS * VA), slice(768 + HEADS * VA, 770 + HEADS * VA))
CONST_W = 770 + HEADS * VA
W_RE, W_IM, W_QKVG, W_O, W_BIAS = (
    slice(0, 128), slice(128, 256), slice(256, 256 + QK + 2 * VW),
    slice(1024, 1280), slice(1280, 1408))
WEIGHT_W = 1408


def macaron_kernel(nc: bass.Bass, xin: bass.AP, weights: bass.AP, consts: bass.AP,
                   rope: bass.AP, floor: bass.AP, out: bass.AP):
    fp32 = mybir.dt.float32
    ALU = mybir.AluOpType
    ACT = mybir.ActivationFunctionType
    AX = mybir.AxisListType

    ctx = ExitStack()
    with ctx:
        def sb(name, shape):
            return ctx.enter_context(nc.sbuf_tensor(name, shape, fp32))

        def bank(name):
            return ctx.enter_context(nc.psum_tensor(name, [128, 512], fp32))

        def sem(name):
            return ctx.enter_context(nc.semaphore(name))

        cst = sb("cst", [128, CONST_W])
        wts = sb("wts", [128, WEIGHT_W])
        rope_t = sb("rope_t", [128, CHUNKS, 2, QK])
        floor_t = sb("floor_t", [128, CHUNKS, HEADS])
        ident = cst[:, IDENT]
        a_t = sb("a_t", [128, 128])
        b_t = sb("b_t", [128, 128])
        m_raw = sb("m_raw", [128, 128])
        m_c = sb("m_c", [128, 128])
        w_c = sb("w_c", [128, QK + 2 * VW])
        half_bias = sb("half_bias", [128, 128])
        neg_half = sb("neg_half", [128, HEADS])
        x_in_t = sb("x_in_t", [128, STEP, 2 * D])
        xb = sb("xb", [128, 2, D])
        x1 = sb("x1", [128, STEP, D])
        x2 = sb("x2", [128, 2, D])
        xb2 = sb("xb2", [128, 2, D])
        x1t = sb("x1t", [128, CHUNK])
        x2t = sb("x2t", [128, CHUNK])
        bn = [sb(f"bn{n}", [128, 6]) for n in range(3)]
        mv = [sb(f"mv{n}", [128, 2]) for n in range(3)]
        ve = [sb(f"ve{n}", [128, 2, 1]) for n in range(3)]
        rs = [sb(f"rs{n}", [128, 2, 1]) for n in range(3)]
        term = sb("term", [128, 2, 2, QK])
        qk = sb("qk", [128, 2, QK])
        v_aug = sb("v_aug", [128, 2, HEADS, VA])
        sg = sb("sg", [128, 2, HEADS, VAL])
        k_t = sb("k_t", [128, CHUNK])
        q_pad = sb("q_pad", [128, 2, CHUNK])
        probs = [sb(f"probs{n}", [128, PAIRS, CHUNK]) for n in range(2)]
        state = sb("state", [128, BATCHES, HEADS * VA])
        d_state = sb("d_state", [128, HEADS * VA])
        osq = sb("osq", [128, HEADS, VAL])
        ssq = sb("ssq", [128, HEADS])
        ms = sb("ms", [128, HEADS])
        den = sb("den", [128, HEADS])
        w8 = sb("w8", [128, HEADS])
        rstd = sb("rstd", [128, HEADS, 1])
        gate = sb("gate", [128, HEADS, VAL])
        y = sb("y", [128, HEADS * VAL])
        y_t = sb("y_t", [128, 2, CHUNK])
        res = sb("res", [128, 2, D])

        ps_qk = bank("ps_qk")
        ps_vg = bank("ps_vg")
        ps_s0 = bank("ps_s0")
        ps_s1 = bank("ps_s1")
        ps_o = bank("ps_o")
        ps_t2 = bank("ps_t2")
        ps_t1 = bank("ps_t1")
        ps_f = bank("ps_f")
        ps_s = [ps_s0, ps_s1]
        o_v = ps_o[:, 0:HEADS * VA].rearrange("p (h d) -> p h d", h=HEADS)

        s_wts, s_cst, s_floor = sem("wts_in"), sem("cst_in"), sem("floor_in")
        s_rope = sem("rope_in")
        s_x = [sem(f"x_in{n}") for n in range(STEP)]
        s_setup_pe, s_setup_act, s_setup_pool = sem("setup_pe"), sem("setup_act"), sem("setup_pool")
        s_setup_dve = sem("setup_dve")
        s_dve_held, s_pe_held = sem("dve_held"), sem("pe_held")
        s_out = [sem(f"out_stored{n}") for n in range(2)]
        (s_f1, s_x1, s_xb, s_x1t_ps, s_x1t, s_qk_ps, s_vg_ps, s_term, s_qk, s_v, s_sg,
         s_qkt_ps, s_qkt, s_o, s_osq, s_ms, s_den, s_w8, s_rstd, s_gate, s_y, s_yt_ps, s_yt,
         s_wo, s_x2, s_xb2, s_x2t_ps, s_x2t, s_st_ps, s_dst, s_st, s_f2, s_res) = [sem(n) for n in (
             "f1_done", "x1_ready", "xb_ready", "x1t_in_psum", "x1t_ready", "qk_in_psum",
             "vg_in_psum", "rope_terms", "qk_ready", "v_ready", "silu_ready", "qkt_in_psum",
             "qkt_ready", "o_done", "o_squares", "o_mean_sq", "den_ready", "w8_ready",
             "rstd_ready", "gate_ready", "y_ready", "yt_in_psum", "yt_ready", "wo_done",
             "x2_ready", "xb2_ready", "x2t_in_psum", "x2t_ready", "dstate_in_psum",
             "dstate_masked", "state_ready", "f2_done", "res_ready")]
        s_sc = [sem(f"scores_done{n}") for n in range(2)]
        s_pair = [sem(f"pair_scored{n}") for n in range(2)]
        s_p = [sem(f"probs_ready{n}") for n in range(2)]
        s_bn = [sem(f"bn_stats{n}") for n in range(3)]
        s_mv = [sem(f"mean_var{n}") for n in range(3)]
        s_ve = [sem(f"var_eps{n}") for n in range(3)]
        s_rs = [sem(f"rstd_norm{n}") for n in range(3)]

        def ge(eng, s, value):
            if not isinstance(value, int) or value > 0:
                eng.wait_ge(s, value)

        def run(eng, slot):
            for i in range(2):
                for u in range(STEP):
                    slot(i, u, lambda lag: i * STEP + u >= lag)
            with eng.Fori(2, CHUNKS) as i:
                for u in range(STEP):
                    slot(i, u, lambda lag: True)
            for u in range(DEPTH):
                slot(CHUNKS, u, lambda lag: u < lag)

        def chunk_of(i, n):
            return i + n // BATCHES

        block = ctx.enter_context(nc.Block())

        @block.sync
        def _(sp):
            sp.dma_start(wts[:], weights).then_inc(s_wts, 16)
            sp.dma_start(cst[:], consts).then_inc(s_cst, 16)
            for n in range(STEP):
                sp.dma_start(x_in_t[:, n, :], xin[n, :, :]).then_inc(s_x[n], 16)
            sp.dma_start(rope_t[:, 0, :, :], rope[0, :, :].rearrange("p (s n) -> p s n", s=2)).then_inc(s_rope, 16)
            sp.dma_start(floor_t[:, :, :], floor).then_inc(s_floor, 16)

            def slot(i, u, loads, stores):
                if loads and u == 0:
                    c = chunk_of(i, 0)
                    sp.wait_ge(s_rope, c * 16 + 16)
                    sp.dma_start(rope_t[:, bass.ds(c + 1, 1), :, :],
                                 rope[bass.ds(c + 1, 1), :, :].rearrange("o p (s n) -> p o s n", s=2)
                                 ).then_inc(s_rope, 16)
                if loads:
                    t = i * STEP + u
                    sp.wait_ge(s_bn[0], t + 1)
                    sp.wait_ge(s_xb, t + 1)
                    sp.wait_ge(s_f1, t + 1)
                    sp.dma_start(x_in_t[:, u, :],
                                 xin[bass.ds(t + STEP, 1), :, :].rearrange("o p n -> (o p) n")
                                 ).then_inc(s_x[u], 16)
                if stores:
                    d = i * STEP + u - 3
                    sp.wait_ge(s_res, d + 1)
                    sp.dma_start(out[bass.ds(d, 1), :, :].rearrange("o p n -> (o p) n"),
                                 res[:, (u - 3) % 2, :]).then_inc(s_out[(u - 3) % 2], 16)

            for i in range(2):
                for u in range(STEP):
                    slot(i, u, True, i * STEP + u >= DEPTH)
            with sp.Fori(2, CHUNKS - 1) as i:
                for u in range(STEP):
                    slot(i, u, True, True)
            for u in range(STEP):
                slot(CHUNKS - 1, u, False, True)
            for u in range(DEPTH):
                slot(CHUNKS, u, False, True)
            for n in range(2):
                sp.wait_ge(s_out[n], 16 * (TILES // 2))

        @block.gpsimd
        def _(pool):
            nc.gpsimd.memset(neg_half[:], -0.5)
            nc.gpsimd.memset(state[:], 0.0)
            nc.gpsimd.memset(v_aug[:, :, :, VAL:VA], 1.0).then_inc(s_setup_pool, 1)
            pool.wait_ge(s_wts, 16)
            nc.gpsimd.tensor_scalar(half_bias[:], wts[:, W_BIAS], 0.5, None,
                                    ALU.mult).then_inc(s_setup_pool, 1)
            pool.wait_ge(s_setup_pool, 2)

            def root(n, t, par):
                pool.wait_ge(s_ve[n], t + 1)
                nc.gpsimd.tensor_tensor(rs[n][:, par, :], ve[n][:, par, :], neg_half[:, 0:1],
                                        ALU.pow).then_inc(s_rs[n], 1)

            def slot(i, u, on):
                a, b, c, d = (i * STEP + u - lag for lag in range(4))
                if on(3):
                    pool.wait_ge(s_w8, d + 1)
                    nc.gpsimd.tensor_tensor(rstd[:, :, 0], w8[:], neg_half[:],
                                            ALU.pow).then_inc(s_rstd, 1)
                    pool.wait_ge(s_rstd, d + 1)
                    pool.wait_ge(s_sg, d + 1)
                    ge(pool, s_y, d)
                    nc.gpsimd.tensor_tensor(gate[:], sg[:, (u - 3) % 2, :, :],
                                            rstd[:].to_broadcast([128, HEADS, VAL]),
                                            ALU.mult).then_inc(s_gate, 1)
                if on(0):
                    ge(pool, s_x1, a - 1)
                    root(0, a, u % 2)
                    pool.wait_ge(s_x[u % STEP], chunk_of(i, u) * 16 + 16)
                    nc.gpsimd.tensor_tensor(xb[:, u % 2, :], x_in_t[:, u % STEP, 0:D],
                                            half_bias[:], ALU.add).then_inc(s_xb, 1)
                    ge(pool, s_sg, a - 1)
                    root(1, a, u % 2)
                if on(1):
                    pool.wait_ge(s_term, b + 1)
                    ge(pool, s_st_ps, b - 1)
                    nc.gpsimd.tensor_tensor(qk[:, (u - 1) % 2, :], term[:, (u - 1) % 2, 0, :],
                                            term[:, (u - 1) % 2, 1, :], ALU.add).then_inc(s_qk, 1)
                if on(3):
                    ge(pool, s_res, d - 1)
                    root(2, d, (u - 3) % 2)
                    pool.wait_ge(s_x2, d + 1)
                    nc.gpsimd.tensor_tensor(xb2[:, (u - 3) % 2, :], x2[:, (u - 3) % 2, :],
                                            half_bias[:], ALU.add).then_inc(s_xb2, 1)
                if on(2):
                    pool.wait_ge(s_dst, c + 1)
                    pool.wait_ge(s_o, c + 1)
                    bt = (u - 2) % BATCHES
                    nc.gpsimd.tensor_tensor(state[:, bt, :], state[:, bt, :], d_state[:],
                                            ALU.add).then_inc(s_st, 1)

            run(pool, slot)

        @block.scalar
        def _(act):
            act.wait_ge(s_setup_pe, 1)
            nc.scalar.copy(a_t[:], ps_qk[:, 0:128])
            nc.scalar.copy(b_t[:], ps_qk[:, 128:256]).then_inc(s_setup_act, 1)
            act.wait_ge(s_setup_pe, 2)
            nc.scalar.mul(m_raw[:], ps_qk[:, 256:384], 0.5 / D).then_inc(s_setup_act, 1)
            act.wait_ge(s_setup_pe, 3)
            nc.scalar.copy(w_c[:, 0:512], ps_vg[:])
            nc.scalar.copy(w_c[:, 512:768], ps_f[:, 0:256]).then_inc(s_setup_act, 1)
            act.wait_ge(s_setup_pe, 4)
            nc.scalar.copy(m_c[:], ps_qk[:, 384:512]).then_inc(s_setup_act, 1)
            act.wait_ge(s_setup_pool, 2)

            def slot(i, u, on):
                a, b, c, d = (i * STEP + u - lag for lag in range(4))
                if on(1):
                    act.wait_ge(s_x1t_ps, b + 1)
                    nc.scalar.copy(x1t[:], ps_t1[:, 0:CHUNK]).then_inc(s_x1t, 1)
                    par = (u - 1) % 2
                    act.wait_ge(s_vg_ps, b + 1)
                    act.wait_ge(s_rs[1], b + 1)
                    ge(act, s_st_ps, b - 1)
                    nc.scalar.activation(v_aug[:, par, :, 0:VAL],
                                         ps_vg[:, 0:VW].rearrange("p (h d) -> p h d", h=HEADS),
                                         ACT.Copy, scale=rs[1][:, par, :]).then_inc(s_v, 1)
                    ge(act, s_gate, b - 1)
                    nc.scalar.activation(sg[:, par, :, :],
                                         ps_vg[:, VW:2 * VW].rearrange("p (h d) -> p h d", h=HEADS),
                                         ACT.Silu, scale=rs[1][:, par, :]).then_inc(s_sg, 1)
                if on(3):
                    act.wait_ge(s_yt_ps, d + 1)
                    nc.scalar.copy(y_t[:], ps_t2[:, 0:256].rearrange("p (n c) -> p n c", n=2)
                                   ).then_inc(s_yt, 1)
                if on(1):
                    act.wait_ge(s_qkt_ps, b + 1)
                    for n in range(2):
                        nc.scalar.activation(q_pad[:, n, :], ps_t2[:, 0:CHUNK], ACT.Copy,
                                             scale=cst[:, PARITY.start + n:PARITY.start + n + 1])
                    nc.scalar.copy(k_t[:], ps_t2[:, CHUNK:2 * CHUNK]).then_inc(s_qkt, 1)
                if on(3):
                    act.wait_ge(s_x2t_ps, d + 1)
                    nc.scalar.copy(x2t[:], ps_t1[:, 0:CHUNK]).then_inc(s_x2t, 1)
                if on(2):
                    act.wait_ge(s_o, c + 1)
                    ge(act, s_w8, c)
                    nc.scalar.activation(osq[:], o_v[:, :, 0:VAL], ACT.Square)
                    nc.scalar.activation(ssq[:], o_v[:, :, VAL], ACT.Square,
                                         scale=RMS_EPS ** 0.5).then_inc(s_osq, 1)

            run(act, slot)

        @block.vector
        def _(dve):
            nc.vector.memset(ps_s0[:], 0.0)
            nc.vector.memset(ps_s1[:], 0.0).then_inc(s_setup_dve, 1)

            def norm(n, src, t, par):
                nc.vector.bn_stats(bn[n][:], src).then_inc(s_bn[n], 1)
                dve.wait_ge(s_bn[n], t + 1)
                dve.sem_inc(s_dve_held, 1)
                nc.vector.bn_aggr(mv[n][:], bn[n][:]).then_inc(s_mv[n], 1)
                dve.wait_ge(s_mv[n], t + 1)
                nc.vector.tensor_scalar(ve[n][:, par, :], mv[n][:, 1:2], LN_EPS, None,
                                        ALU.add).then_inc(s_ve[n], 1)

            def masked(n, c):
                dve.wait_ge(s_sc[n], c + 1)
                nc.vector.tensor_tensor(
                    probs[n][:], ps_s[n][:].rearrange("p (h i) -> p h i", h=PAIRS),
                    cst[:, CAUSAL].rearrange("p (o i) -> p o i", o=1).to_broadcast([128, PAIRS, CHUNK]),
                    ALU.mult).then_inc(s_p[n], 1)

            def slot(i, u, on):
                a, b, c, d = (i * STEP + u - lag for lag in range(4))
                if on(0):
                    dve.wait_ge(s_x[u % STEP], chunk_of(i, u) * 16 + 16)
                    norm(0, x_in_t[:, u % STEP, 0:D], a, u % 2)
                if on(0):
                    dve.wait_ge(s_f1, a + 1)
                    dve.wait_ge(s_rs[0], a + 1)
                    dve.wait_ge(s_xb, a + 1)
                    nc.vector.scalar_tensor_tensor(x1[:, u % STEP, :], ps_f[:, 0:D],
                                                   rs[0][:, u % 2, :], xb[:, u % 2, :],
                                                   ALU.mult, ALU.add).then_inc(s_x1, 1)
                    dve.wait_ge(s_x1, a + 1)
                    norm(1, x1[:, u % STEP, :], a, u % 2)
                if on(2):
                    masked(0, c)
                if on(3):
                    dve.wait_ge(s_gate, d + 1)
                    nc.vector.tensor_tensor(y[:].rearrange("p (h d) -> p h d", h=HEADS),
                                            o_v[:, :, 0:VAL], gate[:], ALU.mult).then_inc(s_y, 1)
                if on(2):
                    masked(1, c)
                if on(1):
                    par = (u - 1) % 2
                    if u == 1 and on(0):
                        dve.wait_ge(s_rope, chunk_of(i, 0) * 16 + 16)
                    ch = chunk_of(i, u - 1)
                    dve.wait_ge(s_qk_ps, b + 1)
                    dve.wait_ge(s_rs[1], b + 1)
                    ge(dve, s_qk, b - 1)
                    src = ps_qk[:, 0:QK]
                    swapped = src.rearrange("p (m two) -> p m two", two=2)[:, :, ::-1]
                    nc.vector.scalar_tensor_tensor(term[:, par, 0, :], src, rs[1][:, par, :],
                                                   rope_t[:, bass.ds(ch, 1), 0, :],
                                                   ALU.mult, ALU.mult)
                    nc.vector.scalar_tensor_tensor(
                        term[:, par, 1, :].rearrange("p (m two) -> p m two", two=2), swapped,
                        rs[1][:, par, :],
                        rope_t[:, bass.ds(ch, 1), 1, :].rearrange("p o (m two) -> p (o m) two", two=2),
                        ALU.mult, ALU.mult).then_inc(s_term, 1)
                if on(3):
                    dve.wait_ge(s_wo, d + 1)
                    nc.vector.tensor_tensor(x2[:, (u - 3) % 2, :], ps_f[:, 0:D],
                                            x1[:, (u - 3) % STEP, :], ALU.add).then_inc(s_x2, 1)
                    dve.wait_ge(s_x2, d + 1)
                    norm(2, x2[:, (u - 3) % 2, :], d, (u - 3) % 2)
                if on(2):
                    dve.wait_ge(s_st_ps, c + 1)
                    ge(dve, s_st, c)
                    nc.vector.tensor_tensor(d_state[:], ps_s0[:, 0:HEADS * VA],
                                            cst[:, BLOCK], ALU.mult).then_inc(s_dst, 1)
                if on(3):
                    dve.wait_ge(s_f2, d + 1)
                    dve.wait_ge(s_rs[2], d + 1)
                    dve.wait_ge(s_xb2, d + 1)
                    ge(dve, s_out[(u - 3) % 2], 16 * (i * (STEP // 2) + (u - 3) // 2))
                    nc.vector.scalar_tensor_tensor(res[:, (u - 3) % 2, :], ps_f[:, 0:D],
                                                   rs[2][:, (u - 3) % 2, :], xb2[:, (u - 3) % 2, :],
                                                   ALU.mult, ALU.add).then_inc(s_res, 1)
                if on(2):
                    dve.wait_ge(s_osq, c + 1)
                    nc.vector.tensor_reduce(ms[:], osq[:], AX.X, ALU.add).then_inc(s_ms, 1)
                    nc.vector.tensor_tensor(
                        den[:], ssq[:],
                        floor_t[:, bass.ds(chunk_of(i, u - 2), 1), :].rearrange("p o h -> p (o h)"),
                        ALU.max).then_inc(s_den, 1)
                    dve.wait_ge(s_ms, c + 1)
                    dve.wait_ge(s_den, c + 1)
                    ge(dve, s_rstd, c)
                    nc.vector.scalar_tensor_tensor(w8[:], ms[:], 1.0 / VAL, den[:],
                                                   ALU.mult, ALU.add).then_inc(s_w8, 1)

            dve.wait_ge(s_cst, 16)
            dve.wait_ge(s_floor, 16)
            run(dve, slot)

        @block.tensor
        def _(pe):
            mm = nc.tensor.matmul
            pe.wait_ge(s_wts, 16)
            pe.wait_ge(s_cst, 16)
            w_re, w_im = wts[:, W_RE], wts[:, W_IM]
            cos_m, sin_m, neg_sin = cst[:, COS_M], cst[:, SIN_M], cst[:, NEG_SIN_M]
            mm(ps_qk[:, 0:128], w_re, cos_m, start=True, stop=False)
            mm(ps_qk[:, 0:128], w_im, sin_m, start=False, stop=True)
            mm(ps_qk[:, 128:256], w_im, cos_m, start=True, stop=False)
            mm(ps_qk[:, 128:256], w_re, neg_sin, start=False, stop=True).then_inc(s_setup_pe, 1)
            pe.wait_ge(s_setup_act, 1)
            mm(ps_qk[:, 256:384], a_t[:], cos_m, start=True, stop=False)
            mm(ps_qk[:, 256:384], b_t[:], neg_sin, start=False, stop=True).then_inc(s_setup_pe, 1)
            mm(ps_vg[:], cst[:, CENTRE], wts[:, W_QKVG.start:W_QKVG.start + 512], start=True, stop=True)
            mm(ps_f[:, 0:256], cst[:, CENTRE], wts[:, W_QKVG.start + 512:W_QKVG.stop],
               start=True, stop=True).then_inc(s_setup_pe, 1)
            pe.wait_ge(s_setup_act, 2)
            mm(ps_qk[:, 384:512], cst[:, CENTRE], m_raw[:], start=True, stop=True).then_inc(s_setup_pe, 1)
            pe.wait_ge(s_setup_act, 4)
            pe.wait_ge(s_setup_dve, 1)
            pe.wait_ge(s_setup_pool, 2)

            def scores(pair):
                ps = ps_s[pair % 2][:].rearrange("p (h i) -> p h i", h=PAIRS)
                rows, at = slice(32 * pair, 32 * pair + 32), 2 * (pair // 2)
                for j in range(0, CHUNK, 32):
                    last = mm(ps[j:j + 32, at:at + 2, j:CHUNK], k_t[rows, j:j + 32],
                              q_pad[rows, :, j:CHUNK], start=True, stop=True)
                return last

            def weigh(n, par):
                for h in range(PAIRS):
                    pair, parity = n + 2 * (h // 2), h % 2
                    at = parity * PAIRS + pair
                    for i in range(0, CHUNK, 64):
                        last = mm(ps_o[i:i + 64, at * VA:(at + 1) * VA], probs[n][:, h, i:i + 64],
                                  v_aug[:, par, at, :], start=False, stop=(n == 1),
                                  skip_group_check=True)
                return last

            def slot(i, u, on):
                a, b, c, d = (i * STEP + u - lag for lag in range(4))
                if on(1):
                    ge(pe, s_x2t, b - 2)
                    pe.wait_ge(s_x1, b + 1)
                    nc.tensor.transpose(ps_t1[:, 0:CHUNK], x1[:, (u - 1) % STEP, :],
                                        ident).then_inc(s_x1t_ps, 1)
                if on(2):
                    ge(pe, s_dst, c)
                    pe.wait_ge(s_qkt, c + 1)
                    ge(pe, s_p[1], c)
                    pe.sem_inc(s_pe_held, 1)
                    scores(0).then_inc(s_pair[0], 1)
                    scores(1).then_inc(s_pair[1], 1)
                if on(0):
                    ge(pe, s_res, a - 3)
                    pe.wait_ge(s_x[u % STEP], chunk_of(i, u) * 16 + 16)
                    mm(ps_f[:, 0:D], x_in_t[:, u % STEP, D:2 * D], m_c[:],
                       start=True, stop=True).then_inc(s_f1, 1)
                if on(2):
                    for n in range(2):
                        pe.wait_ge(s_pair[n], c + 1)
                        pe.sem_inc(s_pe_held, 1)
                        scores(2 + n).then_inc(s_sc[n], 1)
                if on(1):
                    pe.wait_ge(s_x1t, b + 1)
                    ge(pe, s_term, b)
                    mm(ps_qk[:, 0:QK], x1t[:], w_c[:, 0:QK], start=True, stop=True).then_inc(s_qk_ps, 1)
                    ge(pe, s_sg, b)
                    mm(ps_vg[:], x1t[:], w_c[:, QK:], start=True, stop=True).then_inc(s_vg_ps, 1)
                if on(3):
                    pe.wait_ge(s_y, d + 1)
                    ge(pe, s_qkt, d + 2 if not isinstance(d, int) else min(d + 2, TILES))
                    nc.tensor.transpose(ps_t2[:, 0:CHUNK], y[:, 0:128], ident)
                    nc.tensor.transpose(ps_t2[:, CHUNK:2 * CHUNK], y[:, 128:256],
                                        ident).then_inc(s_yt_ps, 1)
                if on(2):
                    ge(pe, s_y, c)
                    ge(pe, s_st, c - 1)
                    bt = (u - 2) % BATCHES
                    half = PAIRS * VA
                    for n in range(2):
                        mm(ps_o[:, n * half:(n + 1) * half], q_pad[:, n, :],
                           state[:, bt, n * half:(n + 1) * half], start=(n == 0), stop=False,
                           skip_group_check=True)
                    pe.wait_ge(s_v, c + 1)
                    pe.wait_ge(s_p[0], c + 1)
                    weigh(0, (u - 2) % 2)
                if on(3):
                    pe.wait_ge(s_yt, d + 1)
                    if on(0):
                        pe.wait_ge(s_x1, a + 1)
                    else:
                        ge(pe, s_res, d)
                    for n in range(2):
                        last = mm(ps_f[:, 0:D], y_t[:, n, :],
                                  wts[:, W_O.start + n * 128:W_O.start + (n + 1) * 128],
                                  start=(n == 0), stop=(n == 1))
                    last.then_inc(s_wo, 1)
                if on(2):
                    pe.wait_ge(s_p[1], c + 1)
                    weigh(1, (u - 2) % 2).then_inc(s_o, 1)
                if on(1):
                    pe.wait_ge(s_qk, b + 1)
                    ge(pe, s_yt, b - 1)
                    nc.tensor.transpose(ps_t2[:, 0:CHUNK], qk[:, (u - 1) % 2, 0:128], ident)
                    nc.tensor.transpose(ps_t2[:, CHUNK:2 * CHUNK], qk[:, (u - 1) % 2, 128:256],
                                        ident).then_inc(s_qkt_ps, 1)
                if on(3):
                    pe.wait_ge(s_x2, d + 1)
                    nc.tensor.transpose(ps_t1[:, 0:CHUNK], x2[:, (u - 3) % 2, :],
                                        ident).then_inc(s_x2t_ps, 1)
                if on(2):
                    mm(ps_s0[:, 0:HEADS * VA], qk[:, (u - 2) % 2, 128:256], v_aug[:, (u - 2) % 2, :, :],
                       start=True, stop=True).then_inc(s_st_ps, 1)
                if on(3):
                    pe.wait_ge(s_x2t, d + 1)
                    mm(ps_f[:, 0:D], x2t[:], m_c[:], start=True, stop=True).then_inc(s_f2, 1)

            run(pe, slot)


def constants():
    f = np.float32
    n = np.arange(D)
    ang = 2.0 * np.pi * ((n[:, None] * n[None, :]) % D) / D
    heads = np.arange(HEADS)
    order = np.concatenate([heads[0::2], heads[1::2]])
    cst = np.zeros((128, CONST_W), f)
    cst[:, COS_M], cst[:, SIN_M], cst[:, NEG_SIN_M] = np.cos(ang), np.sin(ang), -np.sin(ang)
    cst[:, CENTRE] = np.eye(D) - 1.0 / D
    cst[:, IDENT] = np.eye(128)
    cst[:, CAUSAL] = n[:, None] <= n[None, :]
    cst[:, BLOCK] = (n[:, None] // KEY == order[None, :]).repeat(VA, 1)
    cst[:, PARITY] = (n[:, None] // KEY) % 2 == np.arange(2)[None, :]
    lin = np.linspace(0.0, 1.0, KEY // 2).astype(f)
    angle = np.repeat(f(1.0) / np.power(f(10000.0), lin), 2).astype(f)
    pos = np.arange(SEQ, dtype=f)
    turn = (pos[:, None] * angle[None, :]).astype(f).astype(np.float64)
    cos, sin = np.cos(turn), np.sin(turn) * np.where(np.arange(KEY) % 2, 1.0, -1.0)
    decay = np.log1p(-np.power(2.0, -5.0 - heads)).astype(f).astype(np.float64)
    grow = np.exp(pos.astype(np.float64)[:, None] * decay[None, :])
    rope = np.empty((SEQ, 2, 2, HEADS, KEY), np.float64)
    for n_, tab in enumerate((cos, sin)):
        rope[:, n_, 0] = tab[:, None, :] * grow[:, :, None]
        rope[:, n_, 1] = tab[:, None, :] / grow[:, :, None] * KEY ** -0.5
    rope = rope.reshape(CHUNKS, CHUNK, 2 * QK).astype(f)
    rows = np.cumsum(grow, axis=0)[:, order]
    floor = (rows * RMS_EPS).reshape(CHUNKS, CHUNK, HEADS).transpose(1, 0, 2)
    return cst, rope, np.ascontiguousarray(floor).astype(f)


def kernel(L0_attn_x, L0_attn_wq, L0_attn_wk, L0_attn_wv, L0_attn_wg, L0_attn_wo,
           L0_ffn_w_freq_real, L0_ffn_w_freq_imag, L0_ffn_bias):
    import concourse.bacc as bacc
    from concourse.bass_utils import run_bass_kernel_spmd

    def by_parity(w):
        return w.reshape(-1, PAIRS, 2, VAL).transpose(0, 2, 1, 3).reshape(-1, VW)

    x = np.asarray(L0_attn_x).reshape(BATCHES, CHUNKS, CHUNK, D).transpose(1, 0, 2, 3)
    x = x.reshape(TILES, CHUNK, D)
    xin = np.ascontiguousarray(np.concatenate([x, x.transpose(0, 2, 1)], axis=2))
    wo = by_parity(np.asarray(L0_attn_wo).T).T.reshape(2, 128, D).transpose(1, 0, 2).reshape(128, 2 * D)
    weights = np.ascontiguousarray(np.concatenate([
        np.asarray(L0_ffn_w_freq_real), np.asarray(L0_ffn_w_freq_imag),
        np.asarray(L0_attn_wq), np.asarray(L0_attn_wk),
        by_parity(np.asarray(L0_attn_wv)), by_parity(np.asarray(L0_attn_wg)), wo,
        np.repeat(np.asarray(L0_ffn_bias).reshape(1, D), 128, axis=0)], axis=1))
    cst, rope, floor = constants()
    nc = bacc.Bacc("TRN2", target_bir_lowering=False, num_devices=1)
    arrays = {"xin": xin, "weights": weights, "consts": cst, "rope": rope, "row_floor": floor}
    aps = [nc.dram_tensor(n, v.shape, mybir.dt.float32, kind="ExternalInput").ap()
           for n, v in arrays.items()]
    out = nc.dram_tensor("out", (TILES, CHUNK, D), mybir.dt.float32, kind="ExternalOutput").ap()
    macaron_kernel(nc, *aps, out)
    got = run_bass_kernel_spmd(nc, [arrays], core_ids=[0]).results[0]["out"]
    return got.reshape(CHUNKS, BATCHES, CHUNK, D).transpose(1, 0, 2, 3).reshape(BATCHES, SEQ, D)
```

```python
import numpy as np
import concourse.bass as bass
from concourse import mybir
from contextlib import ExitStack

BATCHES, SEQ, D = 4, 1024, 128
HEADS, KEY, VAL = 8, 16, 32
PAIRS = HEADS // 2
CHUNK = 128
CHUNKS = SEQ // CHUNK
TILES = BATCHES * CHUNKS
QK = 2 * HEADS * KEY
VW = HEADS * VAL
VA = VAL + 1
LN_EPS = 1e-5
RMS_EPS = 1e-5
STEP = BATCHES
DEPTH = 5

COS_M, SIN_M, NEG_SIN_M, COS_C, CENTRE, IDENT, CAUSAL, BLOCK, PARITY = (
    slice(0, 128), slice(128, 256), slice(256, 384), slice(384, 512), slice(512, 640),
    slice(640, 768), slice(768, 896), slice(896, 896 + HEADS * VA),
    slice(896 + HEADS * VA, 898 + HEADS * VA))
CONST_A = 512
CONST_W = 898 + HEADS * VA
W_RE, W_IM, W_QKVG, W_O, W_BIAS = (
    slice(0, 128), slice(128, 256), slice(256, 256 + QK + 2 * VW),
    slice(1024, 1280), slice(1280, 1408))
WEIGHT_W = 1408
WARM = 26


def macaron_kernel(nc: bass.Bass, xin: bass.AP, weights: bass.AP, consts: bass.AP,
                   rope: bass.AP, floor: bass.AP, out: bass.AP):
    fp32 = mybir.dt.float32
    ALU = mybir.AluOpType
    ACT = mybir.ActivationFunctionType
    AX = mybir.AxisListType

    ctx = ExitStack()
    with ctx:
        def sb(name, shape):
            return ctx.enter_context(nc.sbuf_tensor(name, shape, fp32))

        def bank(name):
            return ctx.enter_context(nc.psum_tensor(name, [128, 512], fp32))

        def sem(name):
            return ctx.enter_context(nc.semaphore(name))

        cst = sb("cst", [128, CONST_W])
        wts = sb("wts", [128, WEIGHT_W])
        rope_t = sb("rope_t", [128, CHUNKS, 2, QK])
        floor_t = sb("floor_t", [128, CHUNKS, HEADS])
        ident = cst[:, IDENT]
        a_t = sb("a_t", [128, 128])
        b_t = sb("b_t", [128, 128])
        warm = ctx.enter_context(nc.sbuf_tensor("warm", [128, 512], mybir.dt.bfloat16))
        m_c = sb("m_c", [128, 128])
        w_c = sb("w_c", [128, QK + 2 * VW])
        half_bias = sb("half_bias", [128, 128])
        neg_half = sb("neg_half", [128, HEADS])
        x_in_t = sb("x_in_t", [128, STEP, 2 * D])
        xb = sb("xb", [128, 2, D])
        x1 = sb("x1", [128, STEP, D])
        x2 = sb("x2", [128, 2, D])
        xb2 = sb("xb2", [128, 2, D])
        x1t = sb("x1t", [128, CHUNK])
        x2t = sb("x2t", [128, CHUNK])
        bn = [sb(f"bn{n}", [128, 6]) for n in range(3)]
        mv = [sb(f"mv{n}", [128, 2]) for n in range(3)]
        ve = [sb(f"ve{n}", [128, 2, 1]) for n in range(3)]
        rs = [sb(f"rs{n}", [128, 2, 1]) for n in range(3)]
        term = sb("term", [128, 2, 2, QK])
        qk = sb("qk", [128, 2, QK])
        v_aug = sb("v_aug", [128, 2, HEADS, VA])
        sg = sb("sg", [128, 2, HEADS, VAL])
        k_t = sb("k_t", [128, CHUNK])
        q_pad = sb("q_pad", [128, 2, CHUNK])
        probs = [sb(f"probs{n}", [128, PAIRS, CHUNK]) for n in range(2)]
        state = sb("state", [128, BATCHES, HEADS * VA])
        d_state = sb("d_state", [128, HEADS * VA])
        osq = sb("osq", [128, HEADS, VAL])
        ssq = sb("ssq", [128, HEADS])
        ms = sb("ms", [128, HEADS])
        den = sb("den", [128, HEADS])
        w8 = sb("w8", [128, HEADS])
        rstd = sb("rstd", [128, HEADS, 1])
        og = sb("og", [128, 2, HEADS, VAL])
        y = sb("y", [128, HEADS * VAL])
        y_t = sb("y_t", [128, 2, CHUNK])
        res = sb("res", [128, 2, D])

        ps_qk = bank("ps_qk")
        ps_vg = bank("ps_vg")
        ps_s0 = bank("ps_s0")
        ps_s1 = bank("ps_s1")
        ps_o = bank("ps_o")
        ps_t2 = bank("ps_t2")
        ps_t1 = bank("ps_t1")
        ps_f = bank("ps_f")
        ps_s = [ps_s0, ps_s1]
        o_v = ps_o[:, 0:HEADS * VA].rearrange("p (h d) -> p h d", h=HEADS)

        s_wts, s_cst, s_floor = sem("wts_in"), sem("cst_in"), sem("floor_in")
        s_wffn, s_fourier, s_warm = sem("ffn_weights_in"), sem("fourier_in"), sem("warm_ready")
        s_rope = sem("rope_in")
        s_x = [sem(f"x_in{n}") for n in range(STEP)]
        s_setup_pe, s_setup_act, s_setup_pool = sem("setup_pe"), sem("setup_act"), sem("setup_pool")
        s_setup_dve = sem("setup_dve")
        s_dve_held, s_pe_held = sem("dve_held"), sem("pe_held")
        s_out = [sem(f"out_stored{n}") for n in range(2)]
        (s_f1, s_x1, s_xb, s_x1t_ps, s_x1t, s_qk_ps, s_v_ps, s_g_ps, s_term, s_qk, s_v, s_sg,
         s_qkt_ps, s_qkt, s_o, s_osq, s_ms, s_den, s_w8, s_rstd, s_og, s_y, s_yt_ps, s_yt,
         s_wo, s_x2, s_xb2, s_x2t_ps, s_x2t, s_st_ps, s_dst, s_st, s_f2, s_res) = [sem(n) for n in (
             "f1_done", "x1_ready", "xb_ready", "x1t_in_psum", "x1t_ready", "qk_in_psum",
             "v_in_psum", "g_in_psum", "rope_terms", "qk_ready", "v_ready", "silu_ready", "qkt_in_psum",
             "qkt_ready", "o_done", "o_squares", "o_mean_sq", "den_ready", "w8_ready",
             "rstd_ready", "gated", "y_ready", "yt_in_psum", "yt_ready", "wo_done",
             "x2_ready", "xb2_ready", "x2t_in_psum", "x2t_ready", "dstate_in_psum",
             "dstate_masked", "state_ready", "f2_done", "res_ready")]
        s_sc = [sem(f"scores_done{n}") for n in range(2)]
        s_pair = [sem(f"pair_scored{n}") for n in range(2)]
        s_p = [sem(f"probs_ready{n}") for n in range(2)]
        s_bn = [sem(f"bn_stats{n}") for n in range(3)]
        s_mv = [sem(f"mean_var{n}") for n in range(3)]
        s_ve = [sem(f"var_eps{n}") for n in range(3)]
        s_rs = [sem(f"rstd_norm{n}") for n in range(3)]

        def ge(eng, s, value):
            if not isinstance(value, int) or value > 0:
                eng.wait_ge(s, value)

        def upto(t):
            return min(t + 1, TILES) if isinstance(t, int) else t + 1

        def run(eng, slot):
            for s in range(2 * STEP):
                slot(s // STEP, s % STEP, lambda lag: 0 <= s - lag < TILES)
            with eng.Fori(2, CHUNKS) as i:
                for u in range(STEP):
                    slot(i, u, lambda lag: True)
            for s in range(TILES, TILES + DEPTH):
                slot(s // STEP, s % STEP, lambda lag: 0 <= s - lag < TILES)

        def tiles(i, u):
            return [i * STEP + u - lag for lag in range(DEPTH + 1)]

        def chunk_of(i, n):
            return i + n // BATCHES

        block = ctx.enter_context(nc.Block())

        @block.sync
        def _(sp):
            sp.dma_start(cst[:, 0:CONST_A], consts[:, 0:CONST_A]).then_inc(s_fourier, 16)
            for n in range(STEP):
                sp.dma_start(x_in_t[:, n, :], xin[n, :, :]).then_inc(s_x[n], 16)
            sp.dma_start(rope_t[:, 0, :, :],
                         rope[0, :, :].rearrange("p (s n) -> p s n", s=2)).then_inc(s_rope, 16)
            sp.dma_start(floor_t[:, :, :], floor).then_inc(s_floor, 16)

            def slot(i, u, tables, loads, stores):
                _, a, _, _, _, e = tiles(i, u)
                if tables and u == 0:
                    c = chunk_of(i, 0)
                    sp.wait_ge(s_rope, c * 16 + 16)
                    sp.dma_start(rope_t[:, bass.ds(c + 1, 1), :, :],
                                 rope[bass.ds(c + 1, 1), :, :].rearrange("o p (s n) -> p o s n", s=2)
                                 ).then_inc(s_rope, 16)
                if loads:
                    sp.wait_ge(s_bn[0], a + 1)
                    sp.wait_ge(s_xb, a + 1)
                    sp.wait_ge(s_f1, a + 1)
                    at = (u - 1) % STEP
                    sp.dma_start(x_in_t[:, at, :],
                                 xin[bass.ds(a + STEP, 1), :, :].rearrange("o p n -> (o p) n")
                                 ).then_inc(s_x[at], 16)
                if stores:
                    par = (u - 5) % 2
                    sp.wait_ge(s_res, e + 1)
                    sp.dma_start(out[bass.ds(e, 1), :, :].rearrange("o p n -> (o p) n"),
                                 res[:, par, :]).then_inc(s_out[par], 16)

            for s in range(2 * STEP):
                slot(s // STEP, s % STEP, True, s >= 1, s >= DEPTH)
            with sp.Fori(2, CHUNKS - 1) as i:
                for u in range(STEP):
                    slot(i, u, True, True, True)
            for s in range(TILES - STEP, TILES + DEPTH):
                slot(s // STEP, s % STEP, False, s - 1 + STEP < TILES, True)
            for n in range(2):
                sp.wait_ge(s_out[n], 16 * (TILES // 2))

        @block.gpsimd
        def _(pool):
            nc.gpsimd.memset(neg_half[:], -0.5)
            nc.gpsimd.memset(state[:], 0.0)
            nc.gpsimd.memset(v_aug[:, :, :, VAL:VA], 1.0).then_inc(s_setup_pool, 1)
            pool.wait_ge(s_wts, 16)
            nc.gpsimd.tensor_scalar(half_bias[:], wts[:, W_BIAS], 0.5, None,
                                    ALU.mult).then_inc(s_setup_pool, 1)
            pool.wait_ge(s_setup_pool, 2)

            def root(n, t, par):
                pool.wait_ge(s_ve[n], t + 1)
                nc.gpsimd.tensor_tensor(rs[n][:, par, :], ve[n][:, par, :], neg_half[:, 0:1],
                                        ALU.pow).then_inc(s_rs[n], 1)

            def slot(i, u, on):
                p, a, b, c, d, e = tiles(i, u)
                if on(4):
                    ge(pool, s_y, d)
                    pool.wait_ge(s_w8, d + 1)
                    nc.gpsimd.tensor_tensor(rstd[:, :, 0], w8[:], neg_half[:],
                                            ALU.pow).then_inc(s_rstd, 1)
                if on(5):
                    par = (u - 5) % 2
                    ge(pool, s_res, e - 1)
                    root(2, e, par)
                    pool.wait_ge(s_x2, e + 1)
                    nc.gpsimd.tensor_tensor(xb2[:, par, :], x2[:, par, :], half_bias[:],
                                            ALU.add).then_inc(s_xb2, 1)
                if on(2):
                    par = (u - 2) % 2
                    pool.wait_ge(s_term, b + 1)
                    ge(pool, s_st_ps, b - 1)
                    nc.gpsimd.tensor_tensor(qk[:, par, :], term[:, par, 0, :],
                                            term[:, par, 1, :], ALU.add).then_inc(s_qk, 1)
                if on(0):
                    ge(pool, s_x1, p - 1)
                    root(0, p, u % 2)
                    pool.wait_ge(s_x[u % STEP], chunk_of(i, u) * 16 + 16)
                    nc.gpsimd.tensor_tensor(xb[:, u % 2, :], x_in_t[:, u % STEP, 0:D],
                                            half_bias[:], ALU.add).then_inc(s_xb, 1)
                if on(1):
                    ge(pool, s_sg, a - 1)
                    root(1, a, (u - 1) % 2)
                if on(3):
                    pool.wait_ge(s_dst, c + 1)
                    pool.wait_ge(s_o, c + 1)
                    bt = (u - 3) % BATCHES
                    nc.gpsimd.tensor_tensor(state[:, bt, :], state[:, bt, :], d_state[:],
                                            ALU.add).then_inc(s_st, 1)

            run(pool, slot)

        @block.scalar
        def _(act):
            act.dma_start(wts[:, 0:256], weights[:, 0:256]).then_inc(s_wffn, 16)
            act.dma_start(wts[:, 256:], weights[:, 256:]).then_inc(s_wts, 16)
            act.dma_start(cst[:, CONST_A:], consts[:, CONST_A:]).then_inc(s_cst, 16)
            act.wait_ge(s_setup_pe, 1)
            nc.scalar.copy(a_t[:], ps_qk[:, 0:128])
            nc.scalar.copy(b_t[:], ps_qk[:, 128:256]).then_inc(s_setup_act, 1)
            act.wait_ge(s_setup_pe, 2)
            nc.scalar.mul(m_c[:], ps_qk[:, 256:384], 0.5 / D).then_inc(s_setup_act, 1)
            act.wait_ge(s_cst, 16)
            act.wait_ge(s_setup_pe, 3)
            nc.scalar.copy(w_c[:, 0:512], ps_vg[:])
            nc.scalar.copy(w_c[:, 512:768], ps_t2[:, 0:256]).then_inc(s_setup_act, 1)
            act.wait_ge(s_setup_pool, 2)

            def slot(i, u, on):
                p, a, b, c, d, e = tiles(i, u)
                if on(2):
                    act.wait_ge(s_x1t_ps, b + 1)
                if on(5):
                    act.wait_ge(s_x2t_ps, e + 1)
                if on(2):
                    nc.scalar.copy(x1t[:], ps_t1[:, 0:CHUNK]).then_inc(s_x1t, 1)
                if on(5):
                    nc.scalar.copy(x2t[:], ps_t1[:, CHUNK:2 * CHUNK]).then_inc(s_x2t, 1)
                if on(2):
                    par = (u - 2) % 2
                    act.wait_ge(s_v_ps, b + 1)
                    act.wait_ge(s_rs[1], b + 1)
                    ge(act, s_st_ps, b - 1)
                    nc.scalar.activation(v_aug[:, par, :, 0:VAL],
                                         ps_vg[:, 0:VW].rearrange("p (h d) -> p h d", h=HEADS),
                                         ACT.Copy, scale=rs[1][:, par, :]).then_inc(s_v, 1)
                if on(2):
                    act.wait_ge(s_qkt_ps, b + 1)
                if on(4):
                    act.wait_ge(s_yt_ps, d + 1)
                if on(4):
                    nc.scalar.copy(y_t[:], ps_t2[:, 2 * CHUNK:].rearrange("p (n c) -> p n c", n=2)
                                   ).then_inc(s_yt, 1)
                if on(2):
                    for n in range(2):
                        nc.scalar.activation(q_pad[:, n, :], ps_t2[:, 0:CHUNK], ACT.Copy,
                                             scale=cst[:, PARITY.start + n:PARITY.start + n + 1])
                    nc.scalar.copy(k_t[:], ps_t2[:, CHUNK:2 * CHUNK]).then_inc(s_qkt, 1)
                if on(3):
                    act.wait_ge(s_og, c + 1)
                    ge(act, s_w8, c)
                    nc.scalar.activation(osq[:], o_v[:, :, 0:VAL], ACT.Square)
                    nc.scalar.activation(ssq[:], o_v[:, :, VAL], ACT.Square,
                                         scale=RMS_EPS ** 0.5).then_inc(s_osq, 1)
                if on(2):
                    par = (u - 2) % 2
                    act.wait_ge(s_g_ps, b + 1)
                    ge(act, s_og, b - 1)
                    nc.scalar.activation(sg[:, par, :, :],
                                         ps_vg[:, VW:2 * VW].rearrange("p (h d) -> p h d", h=HEADS),
                                         ACT.Silu, scale=rs[1][:, par, :]).then_inc(s_sg, 1)

            run(act, slot)

        @block.vector
        def _(dve):
            nc.vector.memset(warm[:], 1.0).then_inc(s_warm, 1)
            nc.vector.memset(ps_s0[:], 0.0)
            nc.vector.memset(ps_s1[:], 0.0).then_inc(s_setup_dve, 1)

            def stats(n, src):
                nc.vector.bn_stats(bn[n][:], src).then_inc(s_bn[n], 1)

            def aggregate(n, t):
                dve.wait_ge(s_bn[n], t + 1)
                dve.sem_inc(s_dve_held, 1)
                nc.vector.bn_aggr(mv[n][:], bn[n][:]).then_inc(s_mv[n], 1)

            def add_eps(n, t, par):
                dve.wait_ge(s_mv[n], t + 1)
                nc.vector.tensor_scalar(ve[n][:, par, :], mv[n][:, 1:2], LN_EPS, None,
                                        ALU.add).then_inc(s_ve[n], 1)

            def masked(n, c):
                dve.wait_ge(s_sc[n], c + 1)
                nc.vector.tensor_tensor(
                    probs[n][:], ps_s[n][:].rearrange("p (h i) -> p h i", h=PAIRS),
                    cst[:, CAUSAL].rearrange("p (o i) -> p o i", o=1).to_broadcast([128, PAIRS, CHUNK]),
                    ALU.mult).then_inc(s_p[n], 1)

            def slot(i, u, on):
                p, a, b, c, d, e = tiles(i, u)
                if on(5):
                    aggregate(2, e)
                if on(0):
                    dve.wait_ge(s_x[u % STEP], chunk_of(i, u) * 16 + 16)
                    stats(0, x_in_t[:, u % STEP, 0:D])
                if on(5):
                    add_eps(2, e, (u - 5) % 2)
                if on(0):
                    aggregate(0, p)
                if on(2):
                    par, ch = (u - 2) % 2, chunk_of(i, u - 2)
                    if u == 2:
                        dve.wait_ge(s_rope, ch * 16 + 16)
                    dve.wait_ge(s_qk_ps, b + 1)
                    dve.wait_ge(s_rs[1], b + 1)
                    ge(dve, s_qk, b - 1)
                    src = ps_qk[:, 0:QK]
                    swapped = src.rearrange("p (m two) -> p m two", two=2)[:, :, ::-1]
                    nc.vector.scalar_tensor_tensor(term[:, par, 0, :], src, rs[1][:, par, :],
                                                   rope_t[:, bass.ds(ch, 1), 0, :],
                                                   ALU.mult, ALU.mult)
                    nc.vector.scalar_tensor_tensor(
                        term[:, par, 1, :].rearrange("p (m two) -> p m two", two=2), swapped,
                        rs[1][:, par, :],
                        rope_t[:, bass.ds(ch, 1), 1, :].rearrange("p o (m two) -> p (o m) two", two=2),
                        ALU.mult, ALU.mult).then_inc(s_term, 1)
                if on(1):
                    par = (u - 1) % 2
                    dve.wait_ge(s_f1, a + 1)
                    dve.wait_ge(s_rs[0], a + 1)
                    dve.wait_ge(s_xb, a + 1)
                    nc.vector.scalar_tensor_tensor(x1[:, (u - 1) % STEP, :], ps_f[:, 0:D],
                                                   rs[0][:, par, :], xb[:, par, :],
                                                   ALU.mult, ALU.add).then_inc(s_x1, 1)
                if on(0):
                    add_eps(0, p, u % 2)
                if on(3):
                    if isinstance(c, int) and c == 0:
                        dve.wait_ge(s_cst, 16)
                        dve.wait_ge(s_floor, 16)
                    masked(0, c)
                if on(1):
                    dve.wait_ge(s_x1, a + 1)
                    stats(1, x1[:, (u - 1) % STEP, :])
                if on(3):
                    masked(1, c)
                if on(1):
                    aggregate(1, a)
                if on(4):
                    dve.wait_ge(s_rstd, d + 1)
                    ge(dve, s_yt_ps, d)
                    nc.vector.tensor_tensor(y[:].rearrange("p (h d) -> p h d", h=HEADS),
                                            og[:, (u - 4) % 2, :, :],
                                            rstd[:].to_broadcast([128, HEADS, VAL]),
                                            ALU.mult).then_inc(s_y, 1)
                if on(5):
                    par = (u - 5) % 2
                    dve.wait_ge(s_f2, e + 1)
                    dve.wait_ge(s_rs[2], e + 1)
                    dve.wait_ge(s_xb2, e + 1)
                    ge(dve, s_out[par], 16 * (i * (STEP // 2) + (u - 5) // 2))
                    nc.vector.scalar_tensor_tensor(res[:, par, :], ps_f[:, 0:D],
                                                   rs[2][:, par, :], xb2[:, par, :],
                                                   ALU.mult, ALU.add).then_inc(s_res, 1)
                if on(1):
                    add_eps(1, a, (u - 1) % 2)
                if on(3):
                    dve.wait_ge(s_o, c + 1)
                    dve.wait_ge(s_sg, c + 1)
                    nc.vector.tensor_tensor(og[:, (u - 3) % 2, :, :], o_v[:, :, 0:VAL],
                                            sg[:, (u - 3) % 2, :, :], ALU.mult).then_inc(s_og, 1)
                    dve.wait_ge(s_st_ps, c + 1)
                    ge(dve, s_st, c)
                    nc.vector.tensor_tensor(d_state[:], ps_s0[:, 0:HEADS * VA],
                                            cst[:, BLOCK], ALU.mult).then_inc(s_dst, 1)
                if on(4):
                    par = (u - 4) % 2
                    dve.wait_ge(s_wo, d + 1)
                    ge(dve, s_x2t_ps, d - 1)
                    ge(dve, s_xb2, d - 1)
                    nc.vector.tensor_tensor(x2[:, par, :], ps_f[:, 0:D],
                                            x1[:, (u - 4) % STEP, :], ALU.add).then_inc(s_x2, 1)
                if on(3):
                    dve.wait_ge(s_osq, c + 1)
                    nc.vector.tensor_reduce(ms[:], osq[:], AX.X, ALU.add).then_inc(s_ms, 1)
                    nc.vector.tensor_tensor(
                        den[:], ssq[:],
                        floor_t[:, bass.ds(chunk_of(i, u - 3), 1), :].rearrange("p o h -> p (o h)"),
                        ALU.max).then_inc(s_den, 1)
                if on(4):
                    dve.wait_ge(s_x2, d + 1)
                    stats(2, x2[:, (u - 4) % 2, :])
                if on(3):
                    dve.wait_ge(s_ms, c + 1)
                    dve.wait_ge(s_den, c + 1)
                    ge(dve, s_rstd, c)
                    nc.vector.scalar_tensor_tensor(w8[:], ms[:], 1.0 / VAL, den[:],
                                                   ALU.mult, ALU.add).then_inc(s_w8, 1)

            run(dve, slot)

        @block.tensor
        def _(pe):
            mm = nc.tensor.matmul
            pe.wait_ge(s_warm, 1)
            for _ in range(WARM):
                mm(ps_t1[:], warm[:, 0:128], warm[:], start=True, stop=True)
            pe.wait_ge(s_fourier, 16)
            pe.wait_ge(s_wffn, 16)
            w_re, w_im = wts[:, W_RE], wts[:, W_IM]
            cos_m, sin_m, neg_sin, cos_c = (cst[:, n] for n in (COS_M, SIN_M, NEG_SIN_M, COS_C))
            mm(ps_qk[:, 0:128], w_re, cos_c, start=True, stop=False)
            mm(ps_qk[:, 0:128], w_im, sin_m, start=False, stop=True)
            mm(ps_qk[:, 128:256], w_im, cos_c, start=True, stop=False)
            mm(ps_qk[:, 128:256], w_re, neg_sin, start=False, stop=True).then_inc(s_setup_pe, 1)
            pe.wait_ge(s_setup_act, 1)
            mm(ps_qk[:, 256:384], a_t[:], cos_m, start=True, stop=False)
            mm(ps_qk[:, 256:384], b_t[:], neg_sin, start=False, stop=True).then_inc(s_setup_pe, 1)
            pe.wait_ge(s_setup_act, 2)
            pe.wait_ge(s_setup_dve, 1)
            pe.wait_ge(s_setup_pool, 2)

            def centred_projections():
                pe.wait_ge(s_wts, 16)
                pe.wait_ge(s_cst, 16)
                mm(ps_vg[:], cst[:, CENTRE], wts[:, W_QKVG.start:W_QKVG.start + 512],
                   start=True, stop=True)
                mm(ps_t2[:, 0:256], cst[:, CENTRE], wts[:, W_QKVG.start + 512:W_QKVG.stop],
                   start=True, stop=True).then_inc(s_setup_pe, 1)
                pe.wait_ge(s_setup_act, 3)

            def scores(pair):
                ps = ps_s[pair % 2][:].rearrange("p (h i) -> p h i", h=PAIRS)
                rows, at = slice(32 * pair, 32 * pair + 32), 2 * (pair // 2)
                for j in range(0, CHUNK, 32):
                    last = mm(ps[j:j + 32, at:at + 2, j:CHUNK], k_t[rows, j:j + 32],
                              q_pad[rows, :, j:CHUNK], start=True, stop=True)
                return last

            def weigh(n, par):
                for h in range(PAIRS):
                    pair, parity = n + 2 * (h // 2), h % 2
                    at = parity * PAIRS + pair
                    for i in range(0, CHUNK, 32):
                        last = mm(ps_o[i:i + 32, at * VA:(at + 1) * VA], probs[n][:, h, i:i + 32],
                                  v_aug[:, par, at, :], start=False, stop=(n == 1),
                                  skip_group_check=True)
                return last

            def slot(i, u, on):
                p, a, b, c, d, e = tiles(i, u)
                if isinstance(b, int) and b == 0:
                    centred_projections()
                if on(3):
                    pe.wait_ge(s_qkt, c + 1)
                    ge(pe, s_dst, c)
                    pe.sem_inc(s_pe_held, 1)
                    scores(0).then_inc(s_pair[0], 1)
                if on(2):
                    ge(pe, s_x2t, e)
                    pe.wait_ge(s_x1, b + 1)
                    nc.tensor.transpose(ps_t1[:, 0:CHUNK], x1[:, (u - 2) % STEP, :],
                                        ident).then_inc(s_x1t_ps, 1)
                if on(5):
                    pe.wait_ge(s_x2, e + 1)
                    ge(pe, s_x2t, e)
                    nc.tensor.transpose(ps_t1[:, CHUNK:2 * CHUNK], x2[:, (u - 5) % 2, :],
                                        ident).then_inc(s_x2t_ps, 1)
                if on(3):
                    ge(pe, s_p[1], c)
                    pe.sem_inc(s_pe_held, 1)
                    scores(1).then_inc(s_pair[1], 1)
                if on(2):
                    pe.wait_ge(s_x1t, b + 1)
                    ge(pe, s_term, b)
                    mm(ps_qk[:, 0:QK], x1t[:], w_c[:, 0:QK], start=True, stop=True).then_inc(s_qk_ps, 1)
                if on(1):
                    ge(pe, s_x2, upto(e))
                    pe.wait_ge(s_x[(u - 1) % STEP], chunk_of(i, u - 1) * 16 + 16)
                    mm(ps_f[:, 0:D], x_in_t[:, (u - 1) % STEP, D:2 * D], m_c[:],
                       start=True, stop=True).then_inc(s_f1, 1)
                if on(3):
                    for n in range(2):
                        pe.wait_ge(s_pair[n], c + 1)
                        pe.sem_inc(s_pe_held, 1)
                        scores(2 + n).then_inc(s_sc[n], 1)
                if on(2):
                    ge(pe, s_sg, b)
                    mm(ps_vg[:, 0:VW], x1t[:], w_c[:, QK:QK + VW], start=True, stop=True).then_inc(s_v_ps, 1)
                if on(5):
                    pe.wait_ge(s_x2t, e + 1)
                    ge(pe, s_x1, upto(a))
                    mm(ps_f[:, 0:D], x2t[:], m_c[:], start=True, stop=True).then_inc(s_f2, 1)
                if on(3):
                    ge(pe, s_osq, c)
                    ge(pe, s_st, c - 1)
                    bt = (u - 3) % BATCHES
                    half = PAIRS * VA
                    for n in range(2):
                        mm(ps_o[:, n * half:(n + 1) * half], q_pad[:, n, :],
                           state[:, bt, n * half:(n + 1) * half], start=(n == 0), stop=False,
                           skip_group_check=True)
                    pe.wait_ge(s_v, c + 1)
                    for n in range(2):
                        pe.wait_ge(s_p[n], c + 1)
                        last = weigh(n, (u - 3) % 2)
                    last.then_inc(s_o, 1)
                if on(2):
                    pe.wait_ge(s_qk, b + 1)
                    ge(pe, s_yt, upto(d - 1))
                    nc.tensor.transpose(ps_t2[:, 0:CHUNK], qk[:, (u - 2) % 2, 0:128], ident)
                    nc.tensor.transpose(ps_t2[:, CHUNK:2 * CHUNK], qk[:, (u - 2) % 2, 128:256],
                                        ident).then_inc(s_qkt_ps, 1)
                if on(4):
                    pe.wait_ge(s_y, d + 1)
                    ge(pe, s_qkt, upto(b - 1))
                    nc.tensor.transpose(ps_t2[:, 2 * CHUNK:3 * CHUNK], y[:, 0:128], ident)
                    nc.tensor.transpose(ps_t2[:, 3 * CHUNK:4 * CHUNK], y[:, 128:256],
                                        ident).then_inc(s_yt_ps, 1)
                if on(3):
                    mm(ps_s0[:, 0:HEADS * VA], qk[:, (u - 3) % 2, 128:256], v_aug[:, (u - 3) % 2, :, :],
                       start=True, stop=True).then_inc(s_st_ps, 1)
                if on(2):
                    pe.wait_ge(s_v, b + 1)
                    mm(ps_vg[:, VW:], x1t[:], w_c[:, QK + VW:], start=True, stop=True).then_inc(s_g_ps, 1)
                if on(4):
                    pe.wait_ge(s_yt, d + 1)
                    ge(pe, s_x1, upto(a))
                    ge(pe, s_res, upto(e))
                    for n in range(2):
                        last = mm(ps_f[:, 0:D], y_t[:, n, :],
                                  wts[:, W_O.start + n * 128:W_O.start + (n + 1) * 128],
                                  start=(n == 0), stop=(n == 1))
                    last.then_inc(s_wo, 1)

            run(pe, slot)


def constants():
    f = np.float32
    n = np.arange(D)
    ang = 2.0 * np.pi * ((n[:, None] * n[None, :]) % D) / D
    heads = np.arange(HEADS)
    order = np.concatenate([heads[0::2], heads[1::2]])
    cst = np.zeros((128, CONST_W), f)
    cst[:, COS_M], cst[:, SIN_M], cst[:, NEG_SIN_M] = np.cos(ang), np.sin(ang), -np.sin(ang)
    cst[:, CENTRE] = np.eye(D) - 1.0 / D
    cst[:, COS_C] = np.cos(ang)
    cst[0, COS_C] = 0.0
    cst[:, IDENT] = np.eye(128)
    cst[:, CAUSAL] = n[:, None] <= n[None, :]
    cst[:, BLOCK] = (n[:, None] // KEY == order[None, :]).repeat(VA, 1)
    cst[:, PARITY] = (n[:, None] // KEY) % 2 == np.arange(2)[None, :]
    lin = np.linspace(0.0, 1.0, KEY // 2).astype(f)
    angle = np.repeat(f(1.0) / np.power(f(10000.0), lin), 2).astype(f)
    pos = np.arange(SEQ, dtype=f)
    turn = (pos[:, None] * angle[None, :]).astype(f).astype(np.float64)
    cos, sin = np.cos(turn), np.sin(turn) * np.where(np.arange(KEY) % 2, 1.0, -1.0)
    decay = np.log1p(-np.power(2.0, -5.0 - heads)).astype(f).astype(np.float64)
    grow = np.exp(pos.astype(np.float64)[:, None] * decay[None, :])
    rope = np.empty((SEQ, 2, 2, HEADS, KEY), np.float64)
    for n_, tab in enumerate((cos, sin)):
        rope[:, n_, 0] = tab[:, None, :] * grow[:, :, None]
        rope[:, n_, 1] = tab[:, None, :] / grow[:, :, None] * KEY ** -0.5
    rope = rope.reshape(CHUNKS, CHUNK, 2 * QK).astype(f)
    rows = np.cumsum(grow, axis=0)[:, order]
    floor = (rows * RMS_EPS).reshape(CHUNKS, CHUNK, HEADS).transpose(1, 0, 2)
    return cst, rope, np.ascontiguousarray(floor).astype(f)


def kernel(L0_attn_x, L0_attn_wq, L0_attn_wk, L0_attn_wv, L0_attn_wg, L0_attn_wo,
           L0_ffn_w_freq_real, L0_ffn_w_freq_imag, L0_ffn_bias):
    import concourse.bacc as bacc
    from concourse.bass_utils import run_bass_kernel_spmd

    def by_parity(w):
        return w.reshape(-1, PAIRS, 2, VAL).transpose(0, 2, 1, 3).reshape(-1, VW)

    x = np.asarray(L0_attn_x).reshape(BATCHES, CHUNKS, CHUNK, D).transpose(1, 0, 2, 3)
    x = x.reshape(TILES, CHUNK, D)
    xin = np.ascontiguousarray(np.concatenate([x, x.transpose(0, 2, 1)], axis=2))
    wo = by_parity(np.asarray(L0_attn_wo).T).T.reshape(2, 128, D).transpose(1, 0, 2).reshape(128, 2 * D)
    weights = np.ascontiguousarray(np.concatenate([
        np.asarray(L0_ffn_w_freq_real), np.asarray(L0_ffn_w_freq_imag),
        np.asarray(L0_attn_wq), np.asarray(L0_attn_wk),
        by_parity(np.asarray(L0_attn_wv)), by_parity(np.asarray(L0_attn_wg)), wo,
        np.repeat(np.asarray(L0_ffn_bias).reshape(1, D), 128, axis=0)], axis=1))
    cst, rope, floor = constants()
    nc = bacc.Bacc("TRN2", target_bir_lowering=False, num_devices=1)
    arrays = {"xin": xin, "weights": weights, "consts": cst, "rope": rope, "row_floor": floor}
    aps = [nc.dram_tensor(n, v.shape, mybir.dt.float32, kind="ExternalInput").ap()
           for n, v in arrays.items()]
    out = nc.dram_tensor("out", (TILES, CHUNK, D), mybir.dt.float32, kind="ExternalOutput").ap()
    macaron_kernel(nc, *aps, out)
    got = run_bass_kernel_spmd(nc, [arrays], core_ids=[0]).results[0]["out"]
    return got.reshape(CHUNKS, BATCHES, CHUNK, D).transpose(1, 0, 2, 3).reshape(BATCHES, SEQ, D)
```

```python
import numpy as np
import concourse.bass as bass
from concourse import mybir
from contextlib import ExitStack

BATCHES, SEQ, D = 4, 1024, 128
HEADS, KEY, VAL = 8, 16, 32
PAIRS = HEADS // 2
CHUNK = 128
CHUNKS = SEQ // CHUNK
TILES = BATCHES * CHUNKS
QK = 2 * HEADS * KEY
VW = HEADS * VAL
VA = VAL + 1
LN_EPS = 1e-5
RMS_EPS = 1e-5
STEP = BATCHES
DEPTH = 5

COS_M, SIN_M, NEG_SIN_M, COS_C, CENTRE, IDENT, CAUSAL, BLOCK, PARITY = (
    slice(0, 128), slice(128, 256), slice(256, 384), slice(384, 512), slice(512, 640),
    slice(640, 768), slice(768, 896), slice(896, 896 + HEADS * VA),
    slice(896 + HEADS * VA, 898 + HEADS * VA))
CONST_A = 512
CONST_W = 898 + HEADS * VA
W_RE, W_IM, W_QKVG, W_O, W_BIAS = (
    slice(0, 128), slice(128, 256), slice(256, 256 + QK + 2 * VW),
    slice(1024, 1280), slice(1280, 1408))
WEIGHT_W = 1408
WARM = 26


def macaron_kernel(nc: bass.Bass, xin: bass.AP, weights: bass.AP, consts: bass.AP,
                   rope: bass.AP, floor: bass.AP, out: bass.AP):
    fp32 = mybir.dt.float32
    fp32r = mybir.dt.float32r
    ALU = mybir.AluOpType
    ACT = mybir.ActivationFunctionType
    AX = mybir.AxisListType

    ctx = ExitStack()
    with ctx:
        def sb(name, shape, dtype=fp32):
            return ctx.enter_context(nc.sbuf_tensor(name, shape, dtype))

        def bank(name):
            return ctx.enter_context(nc.psum_tensor(name, [128, 512], fp32))

        def sem(name):
            return ctx.enter_context(nc.semaphore(name))

        cst = sb("cst", [128, CONST_W])
        wts = sb("wts", [128, WEIGHT_W])
        rope_t = sb("rope_t", [128, CHUNKS, 2, QK])
        floor_t = sb("floor_t", [128, CHUNKS, HEADS])
        ident = cst[:, IDENT]
        a_t = sb("a_t", [128, 128])
        b_t = sb("b_t", [128, 128])
        warm = sb("warm", [128, 512], mybir.dt.bfloat16)
        ident_r = sb("ident_r", [128, 128], fp32r)
        m_c = sb("m_c", [128, 128])
        w_c = sb("w_c", [128, QK + 2 * VW])
        half_bias = sb("half_bias", [128, 128])
        neg_half = sb("neg_half", [128, HEADS])
        x_in_t = sb("x_in_t", [128, STEP, 2 * D])
        xb = sb("xb", [128, 2, D])
        x1 = sb("x1", [128, 2, D])
        x1_kept = sb("x1_kept", [128, STEP, D])
        x2 = sb("x2", [128, 2, D])
        xb2 = sb("xb2", [128, 2, D])
        x1t = sb("x1t", [128, CHUNK])
        x2t = sb("x2t", [128, CHUNK])
        bn = [sb(f"bn{n}", [128, 6]) for n in range(3)]
        mv = [sb(f"mv{n}", [128, 2]) for n in range(3)]
        ve = [sb(f"ve{n}", [128, 2, 1]) for n in range(3)]
        rs = [sb(f"rs{n}", [128, 2, 1]) for n in range(3)]
        term = sb("term", [128, 2, 2, QK])
        qk = sb("qk", [128, STEP, QK])
        v_aug = sb("v_aug", [128, STEP, HEADS, VA])
        sg = sb("sg", [128, STEP, HEADS, VAL])
        q_t = sb("q_t", [128, 2, CHUNK])
        qk_hl = sb("qk_hl", [128, 2 * PAIRS + 1, 4, 32], fp32r)
        hl_flat = qk_hl[:].rearrange("p n b f -> p (n b f)")
        q_hl = hl_flat[:, 0:512].rearrange("p (n b f) -> p n b f", n=PAIRS, b=4)
        k_hl = hl_flat[:, 544:1056].rearrange("p (n b f) -> p n b f", n=PAIRS, b=4)
        k_st = sb("k_st", [128, PAIRS, CHUNK], fp32r)
        q_st = sb("q_st", [128, PAIRS, 2, CHUNK], fp32r)
        probs = [sb(f"probs{n}", [128, PAIRS, CHUNK]) for n in range(2)]
        state = sb("state", [128, BATCHES, HEADS * VA])
        d_state = sb("d_state", [128, HEADS * VA])
        osq = sb("osq", [128, HEADS, VAL])
        ssq = sb("ssq", [128, HEADS])
        ms = sb("ms", [128, HEADS])
        den = sb("den", [128, HEADS])
        w8 = sb("w8", [128, HEADS])
        rstd = sb("rstd", [128, HEADS, 1])
        og = sb("og", [128, 2, HEADS, VAL])
        y = sb("y", [128, HEADS * VAL])
        y_t = sb("y_t", [128, 2, CHUNK])
        res = sb("res", [128, 2, D])

        ps_f = bank("ps_f")
        ps_vg = bank("ps_vg")
        ps_s0 = bank("ps_s0")
        ps_s1 = bank("ps_s1")
        ps_o = bank("ps_o")
        ps_k = bank("ps_k")
        ps_q = bank("ps_q")
        ps_t = bank("ps_t")
        F_AT = slice(QK, QK + D)
        F1_AT = slice(QK + D, QK + 2 * D)
        ps_s = [ps_s0, ps_s1]
        o_v = ps_o[:, 0:HEADS * VA].rearrange("p (h d) -> p h d", h=HEADS)

        s_wts, s_cst, s_floor = sem("wts_in"), sem("cst_in"), sem("floor_in")
        s_wffn, s_fourier, s_warm = sem("ffn_weights_in"), sem("fourier_in"), sem("warm_ready")
        s_rope = sem("rope_in")
        s_x = [sem(f"x_in{n}") for n in range(STEP)]
        s_setup_pe, s_setup_act, s_setup_pool = sem("setup_pe"), sem("setup_act"), sem("setup_pool")
        s_dve_held, s_pe_held = sem("dve_held"), sem("pe_held")
        s_out = [sem(f"out_stored{n}") for n in range(2)]
        (s_f1, s_x1, s_xb, s_x1t_ps, s_x1t, s_qk_ps, s_vg_ps, s_term, s_qk, s_v, s_sg,
         s_qt_ps, s_qt, s_o, s_osq, s_ms, s_den, s_w8, s_rstd, s_og, s_y, s_yt_ps, s_yt,
         s_wo, s_x2, s_xb2, s_x2t_ps, s_x2t, s_st_ps, s_dst, s_st, s_f2, s_res, s_hi, s_lo, s_kept, s_cross, s_kst_ps, s_qst_ps, s_st_qk) = [sem(n) for n in (
             "f1_done", "x1_ready", "xb_ready", "x1t_in_psum", "x1t_ready", "qk_in_psum",
             "vg_in_psum", "rope_terms", "qk_ready", "v_ready", "silu_ready", "qt_in_psum",
             "qt_ready", "o_done", "o_squares", "o_mean_sq", "den_ready", "w8_ready",
             "rstd_ready", "gated", "y_ready", "yt_in_psum", "yt_ready", "wo_done",
             "x2_ready", "xb2_ready", "x2t_in_psum", "x2t_ready", "dstate_in_psum",
             "dstate_masked", "state_ready", "f2_done", "res_ready", "qk_hi", "qk_lo", "x1_copied", "state_read",
             "kstack_in_psum", "qstack_in_psum", "stacks_ready")]
        s_sc = [sem(f"scores_done{n}") for n in range(2)]
        s_p = [sem(f"probs_ready{n}") for n in range(2)]
        s_bn = [sem(f"bn_stats{n}") for n in range(3)]
        s_mv = [sem(f"mean_var{n}") for n in range(3)]
        s_ve = [sem(f"var_eps{n}") for n in range(3)]
        s_rs = [sem(f"rstd_norm{n}") for n in range(3)]

        def ge(eng, s, value):
            if not isinstance(value, int) or value > 0:
                eng.wait_ge(s, value)

        def upto(t):
            return min(t + 1, TILES) if isinstance(t, int) else t + 1

        def run(eng, slot):
            for s in range(2 * STEP):
                slot(s // STEP, s % STEP, lambda lag: 0 <= s - lag < TILES)
            with eng.Fori(2, CHUNKS) as i:
                for u in range(STEP):
                    slot(i, u, lambda lag: True)
            for s in range(TILES, TILES + DEPTH):
                slot(s // STEP, s % STEP, lambda lag: 0 <= s - lag < TILES)

        def tiles(i, u):
            return [i * STEP + u - lag for lag in range(DEPTH + 1)]

        def chunk_of(i, n):
            return i + n // BATCHES

        block = ctx.enter_context(nc.Block())

        @block.sync
        def _(sp):
            sp.dma_start(cst[:, 0:CONST_A], consts[:, 0:CONST_A]).then_inc(s_fourier, 16)
            for n in range(STEP):
                sp.dma_start(x_in_t[:, n, :], xin[n, :, :]).then_inc(s_x[n], 16)
            sp.dma_start(rope_t[:, 0, :, :],
                         rope[0, :, :].rearrange("p (s n) -> p s n", s=2)).then_inc(s_rope, 16)
            sp.dma_start(floor_t[:, :, :], floor).then_inc(s_floor, 16)

            def slot(i, u, tables, loads, stores):
                _, a, _, _, _, e = tiles(i, u)
                if tables and u == 0:
                    c = chunk_of(i, 0)
                    sp.wait_ge(s_rope, c * 16 + 16)
                    sp.dma_start(rope_t[:, bass.ds(c + 1, 1), :, :],
                                 rope[bass.ds(c + 1, 1), :, :].rearrange("o p (s n) -> p o s n", s=2)
                                 ).then_inc(s_rope, 16)
                if loads:
                    sp.wait_ge(s_bn[0], a + 1)
                    sp.wait_ge(s_xb, a + 1)
                    sp.wait_ge(s_f1, a + 1)
                    at = (u - 1) % STEP
                    sp.dma_start(x_in_t[:, at, :],
                                 xin[bass.ds(a + STEP, 1), :, :].rearrange("o p n -> (o p) n")
                                 ).then_inc(s_x[at], 16)
                if stores:
                    par = (u - 5) % 2
                    sp.wait_ge(s_res, e + 1)
                    sp.dma_start(out[bass.ds(e, 1), :, :].rearrange("o p n -> (o p) n"),
                                 res[:, par, :]).then_inc(s_out[par], 16)

            for s in range(2 * STEP):
                slot(s // STEP, s % STEP, True, s >= 1, s >= DEPTH)
            with sp.Fori(2, CHUNKS - 1) as i:
                for u in range(STEP):
                    slot(i, u, True, True, True)
            for s in range(TILES - STEP, TILES + DEPTH):
                slot(s // STEP, s % STEP, False, s - 1 + STEP < TILES, True)
            for n in range(2):
                sp.wait_ge(s_out[n], 16 * (TILES // 2))

        @block.gpsimd
        def _(pool):
            nc.gpsimd.memset(neg_half[:], -0.5)
            nc.gpsimd.memset(state[:], 0.0)
            nc.gpsimd.memset(v_aug[:, :, :, VAL:VA], 1.0).then_inc(s_setup_pool, 1)
            pool.wait_ge(s_wts, 16)
            nc.gpsimd.tensor_scalar(half_bias[:], wts[:, W_BIAS], 0.5, None,
                                    ALU.mult).then_inc(s_setup_pool, 1)
            pool.wait_ge(s_setup_pool, 2)

            def root(n, t, par):
                pool.wait_ge(s_ve[n], t + 1)
                nc.gpsimd.tensor_tensor(rs[n][:, par, :], ve[n][:, par, :], neg_half[:, 0:1],
                                        ALU.pow).then_inc(s_rs[n], 1)

            def slot(i, u, on):
                p, b, k, c, d, e = tiles(i, u)
                if on(0):
                    pool.wait_ge(s_x[u % STEP], chunk_of(i, u) * 16 + 16)
                    ge(pool, s_x1, p - 1)
                    nc.gpsimd.tensor_tensor(xb[:, u % 2, :], x_in_t[:, u % STEP, 0:D],
                                            half_bias[:], ALU.add).then_inc(s_xb, 1)
                if on(5):
                    par = (u - 5) % 2
                    ge(pool, s_res, e - 1)
                    pool.wait_ge(s_x2, e + 1)
                    nc.gpsimd.tensor_tensor(xb2[:, par, :], x2[:, par, :], half_bias[:],
                                            ALU.add).then_inc(s_xb2, 1)
                if on(4):
                    ge(pool, s_y, d)
                    pool.wait_ge(s_w8, d + 1)
                    nc.gpsimd.tensor_tensor(rstd[:, :, 0], w8[:], neg_half[:],
                                            ALU.pow).then_inc(s_rstd, 1)
                if on(5):
                    ge(pool, s_res, e - 1)
                    root(2, e, (u - 5) % 2)
                if on(0):
                    ge(pool, s_x1, p - 1)
                    root(0, p, u % 2)
                if on(1):
                    pool.wait_ge(s_term, b + 1)
                    ge(pool, s_st_ps, b - 3)
                    nc.gpsimd.tensor_tensor(qk[:, (u - 1) % STEP, :], term[:, (u - 1) % 2, 0, :],
                                            term[:, (u - 1) % 2, 1, :], ALU.add).then_inc(s_qk, 1)
                if on(0):
                    ge(pool, s_sg, p - 1)
                    root(1, p, u % 2)
                if on(3):
                    pool.wait_ge(s_dst, c + 1)
                    pool.wait_ge(s_cross, c + 1)
                    bt = (u - 3) % BATCHES
                    nc.gpsimd.tensor_tensor(state[:, bt, :], state[:, bt, :], d_state[:],
                                            ALU.add).then_inc(s_st, 1)

            run(pool, slot)

        @block.scalar
        def _(act):
            act.dma_start(wts[:, 0:256], weights[:, 0:256]).then_inc(s_wffn, 16)
            act.dma_start(wts[:, 256:], weights[:, 256:]).then_inc(s_wts, 16)
            act.dma_start(cst[:, CONST_A:], consts[:, CONST_A:]).then_inc(s_cst, 16)
            act.wait_ge(s_setup_pe, 1)
            nc.scalar.copy(a_t[:], ps_f[:, 0:128])
            nc.scalar.copy(b_t[:], ps_f[:, 128:256]).then_inc(s_setup_act, 1)
            act.wait_ge(s_setup_pe, 2)
            nc.scalar.mul(m_c[:], ps_f[:, 256:384], 0.5 / D).then_inc(s_setup_act, 1)
            act.wait_ge(s_cst, 16)
            act.wait_ge(s_setup_pe, 3)
            nc.scalar.copy(w_c[:, 0:512], ps_vg[:])
            nc.scalar.copy(w_c[:, 512:768], ps_k[:, 0:256])
            nc.scalar.copy(ident_r[:], ident).then_inc(s_setup_act, 1)
            act.wait_ge(s_setup_pool, 2)

            def slot(i, u, on):
                p, b, k, c, d, e = tiles(i, u)
                if on(1):
                    act.wait_ge(s_vg_ps, b + 1)
                    act.wait_ge(s_rs[1], b + 1)
                    ge(act, s_st_ps, b - 3)
                    nc.scalar.activation(v_aug[:, (u - 1) % STEP, :, 0:VAL],
                                         ps_vg[:, 0:VW].rearrange("p (h d) -> p h d", h=HEADS),
                                         ACT.Copy, scale=rs[1][:, (u - 1) % 2, :]).then_inc(s_v, 1)
                if on(1):
                    act.wait_ge(s_x1, b + 1)
                    ge(act, s_x2, b - 3)
                    nc.scalar.copy(x1_kept[:, (u - 1) % STEP, :],
                                   x1[:, (u - 1) % 2, :]).then_inc(s_kept, 1)
                if on(1):
                    act.wait_ge(s_vg_ps, b + 1)
                    ge(act, s_og, b - 3)
                    nc.scalar.activation(sg[:, (u - 1) % STEP, :, :],
                                         ps_vg[:, VW:2 * VW].rearrange("p (h d) -> p h d", h=HEADS),
                                         ACT.Silu, scale=rs[1][:, (u - 1) % 2, :]).then_inc(s_sg, 1)
                if on(5):
                    act.wait_ge(s_x2t_ps, e + 1)
                    nc.scalar.copy(x2t[:], ps_t[:, CHUNK:2 * CHUNK]).then_inc(s_x2t, 1)
                if on(2):
                    act.wait_ge(s_kst_ps, k + 1)
                    nc.scalar.copy(k_st[:], ps_k[:].rearrange("p (n c) -> p n c", n=PAIRS))
                    act.wait_ge(s_qst_ps, k + 1)
                    for n in range(2):
                        last = nc.scalar.activation(
                            q_st[:, :, n, :], ps_q[:].rearrange("p (n c) -> p n c", n=PAIRS),
                            ACT.Copy, scale=cst[:, PARITY.start + n:PARITY.start + n + 1])
                    last.then_inc(s_st_qk, 1)
                if on(4):
                    act.wait_ge(s_yt_ps, d + 1)
                if on(2):
                    act.wait_ge(s_qt_ps, k + 1)
                if on(4):
                    nc.scalar.copy(y_t[:], ps_t[:, 2 * CHUNK:].rearrange("p (n c) -> p n c", n=2)
                                   ).then_inc(s_yt, 1)
                if on(2):
                    ge(act, s_o, k - 1)
                    nc.scalar.copy(q_t[:, u % 2, :], ps_t[:, 0:CHUNK]).then_inc(s_qt, 1)
                if on(1):
                    act.wait_ge(s_qk, b + 1)
                    ge(act, s_qst_ps, b)
                    nc.scalar.copy(qk_hl[:, 0:2 * PAIRS, 1:3, :],
                                   qk[:, (u - 1) % STEP, :].rearrange("p (n o f) -> p n o f", o=1, f=32)
                                   .to_broadcast([128, 2 * PAIRS, 2, 32])).then_inc(s_hi, 1)
                if on(0):
                    act.wait_ge(s_x1t_ps, p + 1)
                    nc.scalar.copy(x1t[:], ps_t[:, 0:CHUNK]).then_inc(s_x1t, 1)
                if on(3):
                    act.wait_ge(s_og, c + 1)
                    ge(act, s_w8, c)
                    nc.scalar.activation(osq[:], o_v[:, :, 0:VAL], ACT.Square)
                    nc.scalar.activation(ssq[:], o_v[:, :, VAL], ACT.Square,
                                         scale=RMS_EPS ** 0.5).then_inc(s_osq, 1)

            run(act, slot)

        @block.vector
        def _(dve):
            nc.vector.memset(warm[:], 1.0).then_inc(s_warm, 1)

            def stats(n, src):
                nc.vector.bn_stats(bn[n][:], src).then_inc(s_bn[n], 1)

            def aggregate(n, t):
                dve.wait_ge(s_bn[n], t + 1)
                dve.sem_inc(s_dve_held, 1)
                nc.vector.bn_aggr(mv[n][:], bn[n][:]).then_inc(s_mv[n], 1)

            def add_eps(n, t, par):
                dve.wait_ge(s_mv[n], t + 1)
                nc.vector.tensor_scalar(ve[n][:, par, :], mv[n][:, 1:2], LN_EPS, None,
                                        ALU.add).then_inc(s_ve[n], 1)

            def masked(n, c):
                dve.wait_ge(s_sc[n], c + 1)
                nc.vector.tensor_tensor(
                    probs[n][:], ps_s[n][:].rearrange("p (h i) -> p h i", h=PAIRS),
                    cst[:, CAUSAL].rearrange("p (o i) -> p o i", o=1).to_broadcast([128, PAIRS, CHUNK]),
                    ALU.mult).then_inc(s_p[n], 1)

            def slot(i, u, on):
                p, b, k, c, d, e = tiles(i, u)
                if on(4):
                    dve.wait_ge(s_osq, d + 1)
                    nc.vector.tensor_tensor(
                        den[:], ssq[:],
                        floor_t[:, bass.ds(chunk_of(i, u - 4), 1), :].rearrange("p o h -> p (o h)"),
                        ALU.max).then_inc(s_den, 1)
                if on(4):
                    dve.wait_ge(s_osq, d + 1)
                    nc.vector.tensor_reduce(ms[:], osq[:], AX.X, ALU.add).then_inc(s_ms, 1)
                if on(0):
                    dve.wait_ge(s_x[u % STEP], chunk_of(i, u) * 16 + 16)
                    stats(0, x_in_t[:, u % STEP, 0:D])
                if on(4):
                    dve.wait_ge(s_ms, d + 1)
                    dve.wait_ge(s_den, d + 1)
                    ge(dve, s_rstd, d)
                    nc.vector.scalar_tensor_tensor(w8[:], ms[:], 1.0 / VAL, den[:],
                                                   ALU.mult, ALU.add).then_inc(s_w8, 1)
                if on(5):
                    dve.wait_ge(s_x2, e + 1)
                    stats(2, x2[:, (u - 5) % 2, :])
                if on(3):
                    if isinstance(c, int) and c == 0:
                        dve.wait_ge(s_cst, 16)
                        dve.wait_ge(s_floor, 16)
                    masked(0, c)
                if on(0):
                    aggregate(0, p)
                if on(5):
                    aggregate(2, e)
                if on(3):
                    masked(1, c)
                if on(0):
                    add_eps(0, p, u % 2)
                if on(1):
                    par, ch = (u - 1) % 2, chunk_of(i, u - 1)
                    if u == 1:
                        dve.wait_ge(s_rope, ch * 16 + 16)
                    dve.wait_ge(s_qk_ps, b + 1)
                    dve.wait_ge(s_rs[1], b + 1)
                    ge(dve, s_qk, b - 1)
                    src = ps_f[:, 0:QK]
                    swapped = src.rearrange("p (m two) -> p m two", two=2)[:, :, ::-1]
                    nc.vector.scalar_tensor_tensor(term[:, par, 0, :], src, rs[1][:, par, :],
                                                   rope_t[:, bass.ds(ch, 1), 0, :],
                                                   ALU.mult, ALU.mult)
                    nc.vector.scalar_tensor_tensor(
                        term[:, par, 1, :].rearrange("p (m two) -> p m two", two=2), swapped,
                        rs[1][:, par, :],
                        rope_t[:, bass.ds(ch, 1), 1, :].rearrange("p o (m two) -> p (o m) two", two=2),
                        ALU.mult, ALU.mult).then_inc(s_term, 1)
                if on(5):
                    add_eps(2, e, (u - 5) % 2)
                if on(4):
                    dve.wait_ge(s_rstd, d + 1)
                    ge(dve, s_yt_ps, d)
                    nc.vector.tensor_tensor(y[:].rearrange("p (h d) -> p h d", h=HEADS),
                                            og[:, (u - 4) % 2, :, :],
                                            rstd[:].to_broadcast([128, HEADS, VAL]),
                                            ALU.mult).then_inc(s_y, 1)
                if on(3):
                    dve.wait_ge(s_o, c + 1)
                    dve.wait_ge(s_sg, c + 1)
                    nc.vector.tensor_tensor(og[:, (u - 3) % 2, :, :], o_v[:, :, 0:VAL],
                                            sg[:, (u - 3) % STEP, :, :], ALU.mult).then_inc(s_og, 1)
                if on(5):
                    par = (u - 5) % 2
                    dve.wait_ge(s_f2, e + 1)
                    if on(0):
                        dve.wait_ge(s_f1, p + 1)
                    dve.wait_ge(s_rs[2], e + 1)
                    dve.wait_ge(s_xb2, e + 1)
                    ge(dve, s_out[par], 16 * (i * (STEP // 2) + (u - 5) // 2))
                    nc.vector.scalar_tensor_tensor(res[:, par, :], ps_f[:, F_AT],
                                                   rs[2][:, par, :], xb2[:, par, :],
                                                   ALU.mult, ALU.add).then_inc(s_res, 1)
                if on(0):
                    ge(dve, s_kept, p - 1)
                    ge(dve, s_x1t_ps, p - 1)
                    if on(5):
                        dve.wait_ge(s_f2, e + 1)
                    dve.wait_ge(s_f1, p + 1)
                    dve.wait_ge(s_rs[0], p + 1)
                    dve.wait_ge(s_xb, p + 1)
                    nc.vector.scalar_tensor_tensor(x1[:, u % 2, :], ps_f[:, F1_AT],
                                                   rs[0][:, u % 2, :], xb[:, u % 2, :],
                                                   ALU.mult, ALU.add).then_inc(s_x1, 1)
                if on(0):
                    dve.wait_ge(s_x1, p + 1)
                    stats(1, x1[:, u % 2, :])
                if on(3):
                    dve.wait_ge(s_st_ps, c + 1)
                    ge(dve, s_st, c)
                    nc.vector.tensor_tensor(d_state[:], ps_s0[:, 0:HEADS * VA],
                                            cst[:, BLOCK], ALU.mult).then_inc(s_dst, 1)
                if on(0):
                    aggregate(1, p)
                if on(0):
                    add_eps(1, p, u % 2)
                if on(1):
                    dve.wait_ge(s_hi, b + 1)
                    whole = [qk[:, (u - 1) % STEP, n * 128:(n + 1) * 128]
                             .rearrange("p (n o f) -> p n o f", o=1, f=32)
                             .to_broadcast([128, PAIRS, 2, 32]) for n in range(2)]
                    nc.vector.tensor_tensor(k_hl[:, :, 2:4, :], whole[1], k_hl[:, :, 0:2, :],
                                            ALU.subtract)
                    nc.vector.tensor_tensor(q_hl[:, :, 0:4:3, :], whole[0], q_hl[:, :, 1:3, :],
                                            ALU.subtract).then_inc(s_lo, 1)
                if on(4):
                    par = (u - 4) % 2
                    dve.wait_ge(s_wo, d + 1)
                    dve.wait_ge(s_kept, d + 1)
                    ge(dve, s_x2t_ps, d - 1)
                    ge(dve, s_xb2, d - 1)
                    nc.vector.tensor_tensor(x2[:, par, :], ps_f[:, F_AT],
                                            x1_kept[:, (u - 4) % STEP, :], ALU.add).then_inc(s_x2, 1)

            run(dve, slot)

        @block.tensor
        def _(pe):
            mm = nc.tensor.matmul
            pe.wait_ge(s_warm, 1)
            for _ in range(WARM):
                mm(ps_t[:], warm[:, 0:128], warm[:], start=True, stop=True)
            pe.wait_ge(s_fourier, 16)
            pe.wait_ge(s_wffn, 16)
            w_re, w_im = wts[:, W_RE], wts[:, W_IM]
            cos_m, sin_m, neg_sin, cos_c = (cst[:, n] for n in (COS_M, SIN_M, NEG_SIN_M, COS_C))
            mm(ps_f[:, 0:128], w_re, cos_c, start=True, stop=False)
            mm(ps_f[:, 0:128], w_im, sin_m, start=False, stop=True)
            mm(ps_f[:, 128:256], w_im, cos_c, start=True, stop=False)
            mm(ps_f[:, 128:256], w_re, neg_sin, start=False, stop=True).then_inc(s_setup_pe, 1)
            pe.wait_ge(s_setup_act, 1)
            mm(ps_f[:, 256:384], a_t[:], cos_m, start=True, stop=False)
            mm(ps_f[:, 256:384], b_t[:], neg_sin, start=False, stop=True).then_inc(s_setup_pe, 1)
            pe.wait_ge(s_setup_act, 2)
            pe.wait_ge(s_setup_pool, 2)
            pe.wait_ge(s_cst, 16)

            def centred_projections():
                pe.wait_ge(s_wts, 16)
                pe.wait_ge(s_cst, 16)
                mm(ps_vg[:], cst[:, CENTRE], wts[:, W_QKVG.start:W_QKVG.start + 512],
                   start=True, stop=True)
                mm(ps_k[:, 0:256], cst[:, CENTRE], wts[:, W_QKVG.start + 512:W_QKVG.stop],
                   start=True, stop=True).then_inc(s_setup_pe, 1)
                pe.wait_ge(s_setup_act, 3)

            def scores(n):
                for pair in (n, n + 2):
                    last = mm(ps_s[n][:, pair // 2 * 2 * CHUNK:(pair // 2 + 1) * 2 * CHUNK],
                              k_st[:, pair, :], q_st[:, pair, :, :], start=True, stop=True)
                last.then_inc(s_sc[n], 1)

            def stack(ps, src):
                for pair in range(PAIRS):
                    last = mm(ps[:, pair * CHUNK:(pair + 1) * CHUNK],
                              src[:, pair, :, :].rearrange("p b f -> p (b f)"), ident_r[:],
                              start=True, stop=True)
                return last

            def weigh(n, par):
                for h in range(PAIRS):
                    pair, parity = n + 2 * (h // 2), h % 2
                    at = parity * PAIRS + pair
                    for i in range(0, CHUNK, 32):
                        last = mm(ps_o[i:i + 32, at * VA:(at + 1) * VA], probs[n][:, h, i:i + 32],
                                  v_aug[:, par, at, :], start=False, stop=(n == 1),
                                  skip_group_check=True)
                return last

            def bank_free(b, d, e, f):
                ge(pe, s_term, upto(b))
                ge(pe, s_res, upto(e))
                ge(pe, s_x2, upto(d))
                ge(pe, s_x1, upto(f))

            def slot(i, u, on):
                p, b, k, c, d, e = tiles(i, u)
                if isinstance(b, int) and b == 0:
                    centred_projections()
                if on(3):
                    pe.wait_ge(s_st_qk, c + 1)
                    ge(pe, s_dst, c)
                    scores(0)
                    ge(pe, s_p[1], c)
                    scores(1)
                if on(1):
                    pe.wait_ge(s_x1t, b + 1)
                    ge(pe, s_sg, b)
                    mm(ps_vg[:], x1t[:], w_c[:, QK:], start=True, stop=True).then_inc(s_vg_ps, 1)
                    bank_free(b - 1, d - 1, e - 1, p - 1)
                    mm(ps_f[:, 0:QK], x1t[:], w_c[:, 0:QK], start=True, stop=True).then_inc(s_qk_ps, 1)
                if on(3):
                    pe.wait_ge(s_qt, c + 1)
                    ge(pe, s_osq, c)
                    ge(pe, s_st, c - 3)
                    mm(ps_o[:, 0:HEADS * VA], q_t[:, (u - 3) % 2, :], state[:, (u - 3) % BATCHES, :],
                       start=True, stop=False, skip_group_check=True).then_inc(s_cross, 1)
                if on(2):
                    pe.wait_ge(s_lo, k + 1)
                    ge(pe, s_st_qk, k)
                    stack(ps_k, k_hl).then_inc(s_kst_ps, 1)
                if on(5):
                    pe.wait_ge(s_x2, e + 1)
                    ge(pe, s_yt, upto(d - 1))
                    ge(pe, s_qt, upto(k - 1))
                    ge(pe, s_x1t, upto(b))
                    nc.tensor.transpose(ps_t[:, CHUNK:2 * CHUNK], x2[:, (u - 5) % 2, :],
                                        ident).then_inc(s_x2t_ps, 1)
                if on(2):
                    stack(ps_q, q_hl).then_inc(s_qst_ps, 1)
                if on(3):
                    for n in range(2):
                        pe.wait_ge(s_p[n], c + 1)
                        last = weigh(n, (u - 3) % STEP)
                    last.then_inc(s_o, 1)
                if on(2):
                    ge(pe, s_x1t, upto(b))
                    ge(pe, s_x2t, upto(e))
                    nc.tensor.transpose(ps_t[:, 0:CHUNK], qk[:, (u - 2) % STEP, 0:128],
                                        ident).then_inc(s_qt_ps, 1)
                if on(0):
                    pe.wait_ge(s_x[u % STEP], chunk_of(i, u) * 16 + 16)
                    bank_free(b, d - 1, e - 1, p - 1)
                    mm(ps_f[:, F1_AT], x_in_t[:, u % STEP, D:2 * D], m_c[:],
                       start=True, stop=True).then_inc(s_f1, 1)
                if on(5):
                    pe.wait_ge(s_x2t, e + 1)
                    bank_free(b, d - 1, e - 1, p - 1)
                    mm(ps_f[:, F_AT], x2t[:], m_c[:], start=True, stop=True).then_inc(s_f2, 1)
                if on(4):
                    pe.wait_ge(s_y, d + 1)
                    ge(pe, s_x1t, upto(b))
                    ge(pe, s_x2t, upto(e))
                    nc.tensor.transpose(ps_t[:, 2 * CHUNK:3 * CHUNK], y[:, 0:128], ident)
                    nc.tensor.transpose(ps_t[:, 3 * CHUNK:4 * CHUNK], y[:, 128:256],
                                        ident).then_inc(s_yt_ps, 1)
                if on(3):
                    pe.wait_ge(s_v, c + 1)
                    pe.wait_ge(s_p[0], c + 1)
                    mm(ps_s0[:, 0:HEADS * VA], qk[:, (u - 3) % STEP, 128:256],
                       v_aug[:, (u - 3) % STEP, :, :], start=True, stop=True).then_inc(s_st_ps, 1)
                if on(4):
                    pe.wait_ge(s_yt, d + 1)
                    bank_free(b, d - 1, e, p)
                    for n in range(2):
                        last = mm(ps_f[:, F_AT], y_t[:, n, :],
                                  wts[:, W_O.start + n * 128:W_O.start + (n + 1) * 128],
                                  start=(n == 0), stop=(n == 1))
                    last.then_inc(s_wo, 1)
                if on(0):
                    pe.wait_ge(s_x1, p + 1)
                    ge(pe, s_x2t, upto(e))
                    ge(pe, s_yt, upto(d))
                    ge(pe, s_qt, upto(k))
                    nc.tensor.transpose(ps_t[:, 0:CHUNK], x1[:, u % 2, :],
                                        ident).then_inc(s_x1t_ps, 1)

            run(pe, slot)


def constants():
    f = np.float32
    n = np.arange(D)
    ang = 2.0 * np.pi * ((n[:, None] * n[None, :]) % D) / D
    heads = np.arange(HEADS)
    order = np.concatenate([heads[0::2], heads[1::2]])
    cst = np.zeros((128, CONST_W), f)
    cst[:, COS_M], cst[:, SIN_M], cst[:, NEG_SIN_M] = np.cos(ang), np.sin(ang), -np.sin(ang)
    cst[:, CENTRE] = np.eye(D) - 1.0 / D
    cst[:, COS_C] = np.cos(ang)
    cst[0, COS_C] = 0.0
    cst[:, IDENT] = np.eye(128)
    cst[:, CAUSAL] = n[:, None] <= n[None, :]
    cst[:, BLOCK] = (n[:, None] // KEY == order[None, :]).repeat(VA, 1)
    cst[:, PARITY] = (n[:, None] // KEY) % 2 == np.arange(2)[None, :]
    lin = np.linspace(0.0, 1.0, KEY // 2).astype(f)
    angle = np.repeat(f(1.0) / np.power(f(10000.0), lin), 2).astype(f)
    pos = np.arange(SEQ, dtype=f)
    turn = (pos[:, None] * angle[None, :]).astype(f).astype(np.float64)
    cos, sin = np.cos(turn), np.sin(turn) * np.where(np.arange(KEY) % 2, 1.0, -1.0)
    decay = np.log1p(-np.power(2.0, -5.0 - heads)).astype(f).astype(np.float64)
    grow = np.exp(pos.astype(np.float64)[:, None] * decay[None, :])
    rope = np.empty((SEQ, 2, 2, HEADS, KEY), np.float64)
    for n_, tab in enumerate((cos, sin)):
        rope[:, n_, 0] = tab[:, None, :] * grow[:, :, None]
        rope[:, n_, 1] = tab[:, None, :] / grow[:, :, None] * KEY ** -0.5
    rope = rope.reshape(CHUNKS, CHUNK, 2 * QK).astype(f)
    rows = np.cumsum(grow, axis=0)[:, order]
    floor = (rows * RMS_EPS).reshape(CHUNKS, CHUNK, HEADS).transpose(1, 0, 2)
    return cst, rope, np.ascontiguousarray(floor).astype(f)


def kernel(L0_attn_x, L0_attn_wq, L0_attn_wk, L0_attn_wv, L0_attn_wg, L0_attn_wo,
           L0_ffn_w_freq_real, L0_ffn_w_freq_imag, L0_ffn_bias):
    import concourse.bacc as bacc
    from concourse.bass_utils import run_bass_kernel_spmd

    def by_parity(w):
        return w.reshape(-1, PAIRS, 2, VAL).transpose(0, 2, 1, 3).reshape(-1, VW)

    x = np.asarray(L0_attn_x).reshape(BATCHES, CHUNKS, CHUNK, D).transpose(1, 0, 2, 3)
    x = x.reshape(TILES, CHUNK, D)
    xin = np.ascontiguousarray(np.concatenate([x, x.transpose(0, 2, 1)], axis=2))
    wo = by_parity(np.asarray(L0_attn_wo).T).T.reshape(2, 128, D).transpose(1, 0, 2).reshape(128, 2 * D)
    weights = np.ascontiguousarray(np.concatenate([
        np.asarray(L0_ffn_w_freq_real), np.asarray(L0_ffn_w_freq_imag),
        np.asarray(L0_attn_wq), np.asarray(L0_attn_wk),
        by_parity(np.asarray(L0_attn_wv)), by_parity(np.asarray(L0_attn_wg)), wo,
        np.repeat(np.asarray(L0_ffn_bias).reshape(1, D), 128, axis=0)], axis=1))
    cst, rope, floor = constants()
    nc = bacc.Bacc("TRN2", target_bir_lowering=False, num_devices=1)
    arrays = {"xin": xin, "weights": weights, "consts": cst, "rope": rope, "row_floor": floor}
    aps = [nc.dram_tensor(n, v.shape, mybir.dt.float32, kind="ExternalInput").ap()
           for n, v in arrays.items()]
    out = nc.dram_tensor("out", (TILES, CHUNK, D), mybir.dt.float32, kind="ExternalOutput").ap()
    macaron_kernel(nc, *aps, out)
    got = run_bass_kernel_spmd(nc, [arrays], core_ids=[0]).results[0]["out"]
    return got.reshape(CHUNKS, BATCHES, CHUNK, D).transpose(1, 0, 2, 3).reshape(BATCHES, SEQ, D)
```
